# Optimizing a Trainium2 kernel written in Bass

```python
import numpy as np
import jax
import jax.numpy as jnp

def _softmax(x, axis=-1):
    return jax.nn.softmax(x, axis=axis)

def _gelu(x):
    return jax.nn.gelu(x, approximate=True)

def _silu(x):
    return jax.nn.silu(x)

def _sigmoid(x):
    return jax.nn.sigmoid(x)

def _layernorm(x, axis=-1, eps=1e-05):
    m = jnp.mean(x, axis=axis, keepdims=True)
    v = jnp.var(x, axis=axis, keepdims=True)
    return (x - m) / jnp.sqrt(v + eps)

def _scatter_add(tgt, idx, src, axis=0):
    return tgt.at[idx].add(src)

def _segment_sum(src, seg, n):
    return jax.ops.segment_sum(src, seg, n)
kernel_name = 'mk_decoder_preln_d1_seqx_r4_ec436f'

def setup_inputs(seed: int=0):
    np.random.seed(seed)
    _w = jnp.asarray

    def _rec_inputs():
        import jax
        import jax.numpy as jnp
        _rk = jax.random.key(seed)
        x = -0.000125 + 0.9999 * jax.random.normal(jax.random.fold_in(_rk, 1), (32, 128, 512), jnp.float32)
        _lenS = 128 - jax.random.randint(jax.random.fold_in(_rk, 7), (32,), 0, max(1, 128 // 4) + 1, jnp.int32)
        _lenS2 = 128 - jax.random.randint(jax.random.fold_in(_rk, 8), (32,), 0, max(1, 128 // 4) + 1, jnp.int32)
        _ctx_2048P = jax.random.normal(jax.random.fold_in(_rk, 11), (32, 16, 512), jnp.float32)
        _ctx_2048c = jax.random.dirichlet(jax.random.fold_in(_rk, 511), 0.3 * jnp.ones((16,), jnp.float32), (32, 128))
        _ctx_2048t = jnp.einsum('bsk,bkd->bsd', _ctx_2048c, _ctx_2048P)
        _ctx_2048t = _ctx_2048t * jax.lax.rsqrt(jnp.mean(jnp.square(_ctx_2048t)) + 1e-12) * 0.953939
        ctx_2048 = -0.000514642 + 1.00011 * (_ctx_2048t + 0.3 * jax.random.normal(jax.random.fold_in(_rk, 611), (32, 128, 512), jnp.float32))
        _validS = jnp.arange(128)[None, :] < _lenS[:, None]
        _validS2 = jnp.arange(128)[None, :] < _lenS2[:, None]
        _causal = jnp.tril(jnp.ones((128, 128), dtype=bool))
        mask_BxS2_bk0 = jnp.logical_not(jnp.broadcast_to(_validS2[:, :], (32, 128)))
        return (x, ctx_2048, mask_BxS2_bk0)
    x, ctx_2048, mask_BxS2_bk0 = _rec_inputs()

    def _L0_attn_setup():
        import jax, jax.numpy as jnp
        import numpy as np
        EMBED_DIM = 512
        HEAD_DIM = 128
        HALF = HEAD_DIM // 2
        NH2 = EMBED_DIM // HALF
        H = NH2 // 2
        DEPTH = 12
        LAMBDA_INIT = 0.8 - 0.6 * float(np.exp(-0.3 * DEPTH))
        SCALING = HEAD_DIM ** (-0.5)
        BATCH, SEQ = (1, 512)
        EPS = 1e-05

        def _rope_tables(t, dim):
            inv = 1.0 / 10000.0 ** (np.arange(0, dim, 2)[:dim // 2].astype(np.float64) / dim)
            ang = np.outer(np.arange(t), inv)
            return (jnp.asarray(np.cos(ang), jnp.float32), jnp.asarray(np.sin(ang), jnp.float32))

        def _apply_rope(x, cos, sin):
            xr, xi = (x[..., 0::2], x[..., 1::2])
            c = cos[None, :, None, :]
            s = sin[None, :, None, :]
            out = jnp.stack([xr * c - xi * s, xr * s + xi * c], axis=-1)
            return out.reshape(x.shape)
        key = jax.random.key(seed)
        ks = jax.random.split(key, 10)
        wstd = 0.25 / float(np.sqrt(EMBED_DIM))
        return {'x': jax.random.normal(ks[0], (BATCH, SEQ, EMBED_DIM), jnp.float32), 'wq': jax.random.normal(ks[1], (EMBED_DIM, EMBED_DIM), jnp.float32) * wstd, 'wk': jax.random.normal(ks[2], (EMBED_DIM, EMBED_DIM), jnp.float32) * wstd, 'wv': jax.random.normal(ks[3], (EMBED_DIM, EMBED_DIM), jnp.float32) * wstd, 'wout': jax.random.normal(ks[4], (EMBED_DIM, EMBED_DIM), jnp.float32) * wstd, 'lambda_q1': jax.random.normal(ks[5], (HALF,), jnp.float32) * 0.1, 'lambda_q2': jax.random.normal(ks[6], (HALF,), jnp.float32) * 0.1, 'lambda_k1': jax.random.normal(ks[7], (HALF,), jnp.float32) * 0.1, 'lambda_k2': jax.random.normal(ks[8], (HALF,), jnp.float32) * 0.1, 'subln_weight': jnp.ones((2 * HALF,), jnp.float32)}
    _L0_attn_all = _L0_attn_setup()
    _L0_attn_in = {k: v for k, v in _L0_attn_all.items() if k in ('wq', 'wk', 'wv', 'wout', 'lambda_q1', 'lambda_q2', 'lambda_k1', 'lambda_k2', 'subln_weight')}
    del _L0_attn_all

    def _L0_xattn_setup():
        import jax, jax.numpy as jnp
        import numpy as np
        key = jax.random.key(seed)
        k1, k2, k3 = jax.random.split(key, 3)
        B, S, D, M = (8, 512, 512, 128)
        hidden_states = jax.random.normal(k1, (B, S, D), dtype=jnp.float32)
        memory_tokens = jax.random.normal(k2, (B, M, D), dtype=jnp.float32)
        memory_mask = jax.random.randint(k3, (B, M), 0, 2).astype(jnp.bool_)
        return {'hidden_states': hidden_states, 'memory_tokens': memory_tokens, 'memory_mask': memory_mask}
    _L0_xattn_all = _L0_xattn_setup()
    _L0_xattn_in = {k: v for k, v in _L0_xattn_all.items() if k in ()}
    del _L0_xattn_all

    def _L0_ffn_setup():
        import jax, jax.numpy as jnp
        import numpy as np
        NUM_EXPERTS = 128
        NUM_KEPT = 48
        TOP_K = 8
        HIDDEN = 512
        INTER = 192
        CAP = 192
        BATCH, SEQ = (2, 256)
        key = jax.random.key(seed)
        k1, k2, k3, k4 = jax.random.split(key, 4)
        hidden_states = jax.random.normal(k1, (BATCH, SEQ, HIDDEN), jnp.float32)
        gate_weight = jax.random.normal(k2, (NUM_EXPERTS, HIDDEN), jnp.float32) * 0.02
        gate_up_proj = jax.random.normal(k3, (NUM_KEPT, 2 * INTER, HIDDEN), jnp.float32) * 0.02
        down_proj = jax.random.normal(k4, (NUM_KEPT, HIDDEN, INTER), jnp.float32) * 0.02
        o2n = -np.ones(NUM_EXPERTS, np.int32)
        o2n[np.arange(NUM_KEPT) * 2] = np.arange(NUM_KEPT, dtype=np.int32)
        old_to_new = jnp.asarray(o2n)
        return {'hidden_states': hidden_states, 'gate_weight': gate_weight, 'gate_up_proj': gate_up_proj, 'down_proj': down_proj, 'old_to_new': old_to_new}
    _L0_ffn_all = _L0_ffn_setup()
    _L0_ffn_in = {k: v for k, v in _L0_ffn_all.items() if k in ('gate_weight', 'gate_up_proj', 'down_proj', 'old_to_new')}
    del _L0_ffn_all
    return {'x': x, 'ctx_2048': ctx_2048, 'mask_BxS2_bk0': mask_BxS2_bk0, 'L0_attn_wq': _L0_attn_in['wq'], 'L0_attn_wk': _L0_attn_in['wk'], 'L0_attn_wv': _L0_attn_in['wv'], 'L0_attn_wout': _L0_attn_in['wout'], 'L0_attn_lambda_q1': _L0_attn_in['lambda_q1'], 'L0_attn_lambda_q2': _L0_attn_in['lambda_q2'], 'L0_attn_lambda_k1': _L0_attn_in['lambda_k1'], 'L0_attn_lambda_k2': _L0_attn_in['lambda_k2'], 'L0_attn_subln_weight': _L0_attn_in['subln_weight'], 'L0_ffn_gate_weight': _L0_ffn_in['gate_weight'], 'L0_ffn_gate_up_proj': _L0_ffn_in['gate_up_proj'], 'L0_ffn_down_proj': _L0_ffn_in['down_proj'], 'L0_ffn_old_to_new': _L0_ffn_in['old_to_new']}

def reference(x, ctx_2048, mask_BxS2_bk0, L0_attn_wq, L0_attn_wk, L0_attn_wv, L0_attn_wout, L0_attn_lambda_q1, L0_attn_lambda_q2, L0_attn_lambda_k1, L0_attn_lambda_k2, L0_attn_subln_weight, L0_ffn_gate_weight, L0_ffn_gate_up_proj, L0_ffn_down_proj, L0_ffn_old_to_new):
    import jax
    import jax.numpy as jnp

    def _L0_attn_ref(x, wq, wk, wv, wout, lambda_q1, lambda_q2, lambda_k1, lambda_k2, subln_weight):
        import jax, jax.numpy as jnp
        import numpy as np
        EMBED_DIM = 512
        HEAD_DIM = 128
        HALF = HEAD_DIM // 2
        NH2 = EMBED_DIM // HALF
        H = NH2 // 2
        DEPTH = 12
        LAMBDA_INIT = 0.8 - 0.6 * float(np.exp(-0.3 * DEPTH))
        SCALING = HEAD_DIM ** (-0.5)
        BATCH, SEQ = (1, 512)
        EPS = 1e-05

        def _rope_tables(t, dim):
            inv = 1.0 / 10000.0 ** (np.arange(0, dim, 2)[:dim // 2].astype(np.float64) / dim)
            ang = np.outer(np.arange(t), inv)
            return (jnp.asarray(np.cos(ang), jnp.float32), jnp.asarray(np.sin(ang), jnp.float32))

        def _apply_rope(x, cos, sin):
            xr, xi = (x[..., 0::2], x[..., 1::2])
            c = cos[None, :, None, :]
            s = sin[None, :, None, :]
            out = jnp.stack([xr * c - xi * s, xr * s + xi * c], axis=-1)
            return out.reshape(x.shape)
        b, t, e = x.shape
        q = (x @ wq.T).reshape(b, t, NH2, HALF)
        k = (x @ wk.T).reshape(b, t, NH2, HALF)
        v = (x @ wv.T).reshape(b, t, H, 2 * HALF)
        cos, sin = _rope_tables(t, HALF)
        q = _apply_rope(q, cos, sin)
        k = _apply_rope(k, cos, sin)
        q = q.transpose(0, 2, 1, 3)
        k = k.transpose(0, 2, 1, 3)
        v = v.transpose(0, 2, 1, 3)
        scores = jnp.einsum('bhtd,bhsd->bhts', q, k) / SCALING
        probs = jax.nn.softmax(scores, axis=-1)
        lam1 = jnp.exp(jnp.sum(lambda_q1 * lambda_k1))
        lam2 = jnp.exp(jnp.sum(lambda_q2 * lambda_k2))
        lam = lam1 - lam2 + LAMBDA_INIT
        probs = probs.reshape(b, H, 2, t, t)
        diff = probs[:, :, 0] - lam * probs[:, :, 1]
        attn = jnp.einsum('bhts,bhsd->bhtd', diff, v)
        attn = attn * jax.lax.rsqrt(jnp.mean(attn * attn, axis=-1, keepdims=True) + EPS)
        attn = attn * subln_weight
        attn = attn.transpose(0, 2, 1, 3).reshape(b, t, e)
        return attn @ wout.T

    def _L0_xattn_ref(hidden_states, memory_tokens, memory_mask):
        import jax, jax.numpy as jnp
        import numpy as np
        B, S, D = hidden_states.shape
        scale = 1.0 / jnp.sqrt(jnp.asarray(D, hidden_states.dtype))
        scores = jnp.einsum('bsd,bmd->bsm', hidden_states, memory_tokens) * scale
        neg_inf = jnp.asarray(-1e+30, scores.dtype)
        scores = jnp.where(memory_mask[:, None, :], scores, neg_inf)
        attn = jax.nn.softmax(scores, axis=-1)
        readout = jnp.einsum('bsm,bmd->bsd', attn, memory_tokens)
        valid_b = jnp.any(memory_mask, axis=-1)
        out = jnp.where(valid_b[:, None, None], readout, jnp.zeros_like(readout))
        return out

    def _L0_ffn_ref(hidden_states, gate_weight, gate_up_proj, down_proj, old_to_new):
        import jax, jax.numpy as jnp
        import numpy as np
        NUM_EXPERTS = 128
        NUM_KEPT = 48
        TOP_K = 8
        HIDDEN = 512
        INTER = 192
        CAP = 192
        BATCH, SEQ = (2, 256)
        B, S, H = hidden_states.shape
        x = hidden_states.reshape(-1, H)
        T = x.shape[0]
        logits = x @ gate_weight.T
        logits = jnp.where(old_to_new[None, :] == -1, -jnp.inf, logits)
        probs = jax.nn.softmax(logits.astype(jnp.float32), axis=-1).astype(logits.dtype)
        top_v, top_i = jax.lax.top_k(probs, TOP_K)
        top_v = top_v / jnp.sum(top_v, axis=-1, keepdims=True)
        sel_new = old_to_new[top_i]
        E = gate_up_proj.shape[0]
        flat_e = sel_new.reshape(-1)
        flat_w = top_v.reshape(-1)
        tok = jnp.repeat(jnp.arange(T), TOP_K)
        oh = (flat_e[:, None] == jnp.arange(E)[None, :]).astype(jnp.int32)
        pos = jnp.sum(jnp.cumsum(oh, axis=0) * oh, axis=-1) - 1
        valid = pos < CAP
        pos_c = jnp.where(valid, pos, CAP)
        xb = jnp.zeros((E, CAP + 1, H), x.dtype).at[flat_e, pos_c].set(x[tok])
        xb = xb[:, :CAP]
        gu = jnp.einsum('ech,eoh->eco', xb, gate_up_proj)
        g, u = jnp.split(gu, 2, axis=-1)
        h = jax.nn.silu(g) * u
        out = jnp.einsum('eci,ehi->ech', h, down_proj)
        y = out[flat_e, jnp.minimum(pos_c, CAP - 1)]
        w = flat_w * valid.astype(flat_w.dtype)
        final = jnp.zeros_like(x).at[tok].add(y * w[:, None])
        return final.reshape(B, S, H)
    x = x + _L0_attn_ref(_layernorm(x, axis=-1), L0_attn_wq, L0_attn_wk, L0_attn_wv, L0_attn_wout, L0_attn_lambda_q1, L0_attn_lambda_q2, L0_attn_lambda_k1, L0_attn_lambda_k2, L0_attn_subln_weight)
    x = x + _L0_xattn_ref(_layernorm(x, axis=-1), ctx_2048, mask_BxS2_bk0)
    x = x + _L0_ffn_ref(_layernorm(x, axis=-1), L0_ffn_gate_weight, L0_ffn_gate_up_proj, L0_ffn_down_proj, L0_ffn_old_to_new)
    return x

_drawn_inputs = setup_inputs


def setup_inputs(seed=0):
    import zlib

    import numpy as np

    out = dict(_drawn_inputs(seed))
    spreads = {'L0_attn_subln_weight': (1.0, 0.2)}
    factors = {'L0_attn_lambda_q1': 2.78,
     'L0_attn_lambda_k2': 3.107,
     'L0_ffn_gate_weight': 8.0,
     'L0_ffn_gate_up_proj': 8.0,
     'L0_ffn_down_proj': 8.0}
    for name, (base, spread) in spreads.items():
        noise = np.random.default_rng([zlib.crc32(name.encode()), seed]).standard_normal(out[name].shape)
        drawn = base * np.exp(spread * noise) if base else spread * noise
        out[name] = jnp.asarray(drawn.astype(out[name].dtype))
    for name, factor in factors.items():
        out[name] = (out[name] * factor).astype(out[name].dtype)
    return out
```

```python
import math
from contextlib import ExitStack

import numpy as np

import concourse.bass as bass
from concourse import mybir

FP32 = mybir.dt.float32
BF16 = mybir.dt.bfloat16
I32 = mybir.dt.int32
U8 = mybir.dt.uint8
ALU = mybir.AluOpType
ACT = mybir.ActivationFunctionType
AX = mybir.AxisListType

P = 128
NB = 32
DM = 512
KC = DM // P
NH2 = 8
HALF = 64
NF = HALF // 2
H = NH2 // 2
M = 128
NEXP = 128
E = 48
INTER = 192
CAP = 192
HS = CAP // 2
T = NB * P
EPS = 1e-5
INV_SCALING = float(P) ** 0.5
XSCALE = float(DM) ** -0.5
LAMBDA_INIT = 0.8 - 0.6 * math.exp(-0.3 * 12)
BIG = 1e30
ROW = DM + E
SLOTS = HS * 2 * E


class Batch:

    def __init__(self, pair, off, limit):
        self.pair, self.off, self.limit = pair, off, limit
        self.parity = off % 2
        self.half = pair + off // 2
        self.index = 2 * pair + off

    def exists(self):
        return not isinstance(self.pair, int) or 0 <= self.index < self.limit

    def back(self, n):
        return Batch(self.pair, self.off - n, self.limit)


class Steps:

    def __init__(self, sem, names):
        self.sem, self.names = sem, names.split()

    def after(self, b, name):
        return len(self.names) * b.index + self.names.index(name) + 1


def wait(eng, steps, b, name):
    if b.exists():
        eng.wait_ge(steps.sem, steps.after(b, name))


def wait_dma(eng, sems, b, per_batch):
    if b.exists():
        eng.wait_ge(sems[b.parity], b.half * (16 * per_batch) + 16 * per_batch)


def decoder_layer(nc, x, ctx_rows, ctx_t, mask, wqk, wv, wout, lambdas, subln, gate, gate_up, down_proj,
                  old_to_new, cos_sin, out):
    xw = nc.dram_tensor("normed_rows_and_weights", (T + CAP, ROW), FP32, kind="Internal").ap()
    table = nc.dram_tensor("token_of_slot", (SLOTS, 1), I32, kind="Internal").ap()

    stack = ExitStack()
    with stack:
        def sb(name, shape, dt=FP32):
            return stack.enter_context(nc.sbuf_tensor(name, shape, dt))

        def sem(name):
            return stack.enter_context(nc.semaphore(name))

        wqk_sb = sb("wqk_sb", [P, KC, 2 * DM])
        wv_sb = sb("wv_sb", [P, KC, DM])
        wout_sb = sb("wout_sb", [P, H, DM])
        gate_sb = sb("gate_sb", [NEXP, DM])
        gate_new = sb("gate_new", [P, KC, E])
        rope_tab = sb("rope_tab", [P, 2, NF])
        lam_in = sb("lam_in", [P, 4, HALF])
        lam_prod = sb("lam_prod", [P, 2, HALF])
        lam_sum = sb("lam_sum", [P, 2])
        lam_exp = sb("lam_exp", [P, 2])
        lam_gap = sb("lam_gap", [P, 1])
        neg_lam = sb("neg_lam", [P, 1])
        subln_sb = sb("subln_sb", [P, 1])
        mask_sb = sb("mask_sb", [P, NB * M], U8)
        valid = sb("valid", [P, NB])
        ident = sb("ident", [P, P])
        ones = sb("ones", [P, P])
        ones_bf = sb("ones_bf", [P, P], BF16)
        before_bf = sb("before_bf", [P, P], BF16)
        neg_half = sb("neg_half", [P, H])
        zeros = sb("zeros", [HS, 2 * ROW])
        o2n_i = sb("o2n_i", [NEXP, 1], I32)
        o2n_f = sb("o2n_f", [NEXP, 1])
        expert_iota = sb("expert_iota", [P, E])
        is_new = sb("is_new", [NEXP, E])
        absent_bias = sb("absent_bias", [P, E])
        slot_base = sb("slot_base", [P, E])
        token_ids = sb("token_ids", [P, NB], I32)
        spare_ids = sb("spare_ids", [HS, E, 2], I32)

        x_ln = sb("x_ln", [P, 2, DM])
        st1 = sb("st1", [P, 6])
        mv1 = sb("mv1", [P, 2])
        rstd1 = sb("rstd1", [P, 1])
        xn1 = sb("xn1", [P, 2, DM])
        xn1_t = sb("xn1_t", [P, KC, P])
        qk_cos = sb("qk_cos", [P, 2 * NH2, 2, NF])
        qk_sin = sb("qk_sin", [P, 2 * NH2, 2, NF])
        qk_rot = sb("qk_rot", [P, 2 * NH2, 2, NF])
        q_t = sb("q_t", [P, H, P])
        k_t = sb("k_t", [P, H, P])
        v_sb = sb("v_sb", [P, 2, DM])
        neg_max = sb("neg_max", [P, 2, H])
        neg_max_s = sb("neg_max_s", [P, 2, H])
        probs = sb("probs", [P, 2, H, P])
        prob_sum = sb("prob_sum", [P, 2, H])
        coef = sb("coef", [P, 2, H])
        weighted = sb("weighted", [P, 2, H, P])
        diff = sb("diff", [P, H, P])
        diff_t = sb("diff_t", [P, H, P])
        squares = sb("squares", [P, H, P])
        sq_sum = sb("sq_sum", [P, H])
        sq_mean = sb("sq_mean", [P, H])
        rstd_h = sb("rstd_h", [P, H])
        heads = sb("heads", [P, H, P])
        heads_t = sb("heads_t", [P, H, P])
        x_res = sb("x_res", [P, 2, DM])
        x1 = sb("x1", [P, 2, DM])
        st2 = sb("st2", [P, 6])
        mv2 = sb("mv2", [P, 2])
        rstd2 = sb("rstd2", [P, 1])
        xn2 = sb("xn2", [P, DM])
        xn2_t = sb("xn2_t", [P, KC, P])
        ctx_sb = sb("ctx_sb", [M, 2, DM])
        ctx_t_sb = sb("ctx_t_sb", [P, 2, KC, M])
        mask_bias = sb("mask_bias", [P, M])
        xscore_kept = sb("xscore_kept", [P, M])
        xscore = sb("xscore", [P, M])
        xneg_max = sb("xneg_max", [P, 1])
        xshifted = sb("xshifted", [P, M])
        xprobs = sb("xprobs", [P, M])
        xsum = sb("xsum", [P, 1])
        xprobs_t = sb("xprobs_t", [M, P])
        xinv = sb("xinv", [P, 1])
        xcoef = sb("xcoef", [P, 1])
        x2 = sb("x2", [P, 2, DM])
        st3 = sb("st3", [P, 6])
        mv3 = sb("mv3", [P, 2])
        rstd3 = sb("rstd3", [P, 1])
        row = sb("row", [P, 2, ROW])
        xn3_t = sb("xn3_t", [P, KC, P])
        logits = sb("logits", [P, E])
        top8 = sb("top8", [P, 8])
        rest = sb("rest", [P, E])
        chosen = sb("chosen", [P, E], BF16)
        lneg_max = sb("lneg_max", [P, 1])
        lexp = sb("lexp", [P, E])
        lexp_chosen = sb("lexp_chosen", [P, E])
        wsum = sb("wsum", [P, 1])
        winv = sb("winv", [P, 1])
        taken = sb("taken", [P, E])
        pos = sb("pos", [P, E])
        fits = sb("fits", [P, E])
        second_half = sb("second_half", [P, E])
        address = sb("address", [P, E])
        address2 = sb("address2", [P, E])
        key = sb("key", [P, E])
        slot8 = sb("slot8", [P, 8])
        no_slot = sb("no_slot", [P, 8])
        slot_idx = sb("slot_idx", [P, 2, 8], I32)
        token_id = sb("token_id", [P, 2], I32)

        gu_sb = sb("gu_sb", [P, 2, KC, 2 * INTER])
        dn_sb = sb("dn_sb", [P, 2, DM])
        dn2_sb = sb("dn2_sb", [INTER - P, 2, DM])
        slot_table = sb("slot_table", [HS, E * 2], I32)
        gather_idx = sb("gather_idx", [HS, 2, 2], I32)
        scatter_idx = sb("scatter_idx", [HS, 2, 2], I32)
        rows = sb("rows", [HS, 2, 2, ROW])
        weight_of = [sb("weight_even", [HS, 2]), sb("weight_odd", [HS, 2])]
        rows_t = sb("rows_t", [P, 2, KC, CAP])
        silu1 = sb("silu1", [P, CAP])
        silu2 = sb("silu2", [INTER - P, CAP])
        h1 = sb("h1", [P, 2, CAP])
        h2 = sb("h2", [INTER - P, 2, CAP])
        y = sb("y", [HS, 2, 2, DM])

        ps = stack.enter_context(nc.psum_tensor("ps", [P, 8, DM], FP32))
        bank_ta, bank_tb = ps[:, 0, :], ps[:, 1, :]
        banks_qk = ps[:, 2:4, :]
        bank_v = ps[:, 4, :]
        bank_o = ps[:, 5, :]
        banks_s = ps[:, 6:8, :]

        def blocks(bank):
            return bank.rearrange("p (c n) -> p c n", n=P)

        s_blank = sem("constants_filled")
        s_made = sem("constants_made")
        s_weights = sem("weights_loaded")
        s_late = sem("late_weights_loaded")
        s_setup_v = sem("setup_by_vector")
        s_setup_pe = sem("setup_by_tensor")
        s_setup_act = sem("setup_by_scalar")
        s_spare = sem("spare_rows_written")
        d_xln = [sem("x_for_norm_loaded0"), sem("x_for_norm_loaded1")]
        d_xres = [sem("x_residual_loaded0"), sem("x_residual_loaded1")]
        d_ctx = [sem("context_loaded0"), sem("context_loaded1")]
        d_row = [sem("records_stored0"), sem("records_stored1")]
        d_x2 = [sem("residual_stored0"), sem("residual_stored1")]
        d_slot = [sem("slots_scattered0"), sem("slots_scattered1")]
        ln1 = Steps(sem("norm1_vector"), "stats aggr eps normed")
        ln1_p = Steps(sem("norm1_pool"), "rstd")
        prj_t = Steps(sem("project_tensor"), "xT qk v qT kT")
        prj_a = Steps(sem("project_scalar"), "xT v qT kT")
        rope = Steps(sem("rope_vector"), "cos sin real imag")
        att_t = Steps(sem("attend_tensor"), "scores diffT pv headsT proj")
        att_a = Steps(sem("attend_scalar"), "exp diffT square headsT")
        att_v = Steps(sem("attend_vector"), "max negmax inv coef weighted diff sqsum sqmean heads")
        att_p = Steps(sem("attend_pool"), "rstd")
        crs_v = Steps(sem("cross_vector"), "x1 stats aggr eps normed bias kept score max shifted")
        crs_p = Steps(sem("cross_pool"), "rstd")
        crs_t = Steps(sem("cross_tensor"), "xT scores probsT readout")
        crs_a = Steps(sem("cross_scalar"), "xT exp probsT")
        out_v = Steps(sem("readout_vector"), "inv coef x2 stats aggr eps normed")
        out_p = Steps(sem("readout_pool"), "rstd")
        rte_t = Steps(sem("route_tensor"), "xT logits counts")
        rte_a = Steps(sem("route_scalar"), "xT exp")
        rte_v = Steps(sem("route_vector"), "logits top8 rest chosen negmax wsum winv weights "
                                           "pos fits half addr addr2 taken key slot8 none slots token")
        d_gu = [sem("gate_up_loaded0"), sem("gate_up_loaded1")]
        d_dn = [sem("down_loaded0"), sem("down_loaded1")]
        s_table = sem("slot_table_loaded")
        d_rows = [sem("rows_gathered0"), sem("rows_gathered1")]
        d_add = [sem("outputs_added0"), sem("outputs_added1")]
        ffn_t = Steps(sem("expert_tensor"), "rowsT0 rowsT1")
        gup_t = Steps(sem("gate_up_tensor"), "first second")
        dwn_t = Steps(sem("down_tensor"), "y0 y1")
        ffn_v = Steps(sem("expert_vector_gather"), "index weight rowsT1")
        ffn_a = Steps(sem("expert_scalar_rows"), "rowsT0")
        gup_a = Steps(sem("gate_up_scalar"), "silu1 silu2")
        gup_v = Steps(sem("gate_up_vector"), "h1 h2")
        dwn_v = Steps(sem("down_vector"), "index y1")
        dwn_a = Steps(sem("down_scalar"), "y0")

        block = stack.enter_context(nc.Block())

        SKEW = {"norm": 0, "project": 1, "attend": 2, "cross": 3, "route": 4}
        PAIRS, FIRST, LAST = (NB + 4) // 2, 3, NB // 2

        def turns(eng, turn):
            def trip(pair):
                for j in range(2):
                    turn({k: Batch(pair, j - s, NB) for k, s in SKEW.items()})
            for pair in range(FIRST):
                trip(pair)
            with eng.Fori(FIRST, LAST) as pair:
                trip(pair)
            for pair in range(LAST, PAIRS):
                trip(pair)

        ESKEW = {"gather": 0, "up": 1, "down": 2}
        EPAIRS, EFIRST, ELAST = (E + 2) // 2, 2, E // 2

        def expert_turns(eng, turn):
            def trip(pair):
                for j in range(2):
                    turn({k: Batch(pair, j - s, E) for k, s in ESKEW.items()})
            for pair in range(EFIRST):
                trip(pair)
            with eng.Fori(EFIRST, ELAST) as pair:
                trip(pair)
            for pair in range(ELAST, EPAIRS):
                trip(pair)

        s_paced = {nc.vector.engine: sem("vector_paced"), nc.gpsimd.engine: sem("pool_paced"),
                   nc.scalar.engine: sem("scalar_paced")}

        def settled(eng):
            eng.sem_inc(s_paced[eng.engine], 1)

        @block.sync
        def _(sp):
            sp.dma_start(wqk_sb[:, :, :], wqk).then_inc(s_weights, 16)
            sp.dma_start(wv_sb[:, :, :], wv).then_inc(s_weights, 16)
            sp.dma_start(rope_tab[:, :, :], cos_sin).then_inc(s_weights, 16)

            def turn(b):
                n, c, r = b["norm"], b["cross"], b["route"]
                if n.exists():
                    wait(sp, ln1, n.back(2), "normed")
                    sp.dma_start(x_ln[:, n.parity, :], x[bass.ds(n.index * P, P), :])\
                      .then_inc(d_xln[n.parity], 16)
                if c.exists():
                    wait(sp, crs_v, c.back(2), "x1")
                    sp.dma_start(x_res[:, c.parity, :], x[bass.ds(c.index * P, P), :])\
                      .then_inc(d_xres[c.parity], 16)
                    wait(sp, crs_t, c.back(2), "readout")
                    sp.dma_start(ctx_t_sb[:, c.parity, :, :], ctx_t[bass.ds(c.index * P, P), :, :])\
                      .then_inc(d_ctx[c.parity], 16)
                    sp.dma_start(ctx_sb[:, c.parity, :], ctx_rows[bass.ds(c.index * M, M), :])\
                      .then_inc(d_ctx[c.parity], 16)
                if r.exists():
                    wait(sp, out_v, r, "x2")
                    sp.dma_start(out[bass.ds(r.index * P, P), :], x2[:, r.parity, :])\
                      .then_inc(d_x2[r.parity], 16)
                    wait(sp, rte_v, r, "weights")
                    sp.dma_start(xw[bass.ds(r.index * P, P), :], row[:, r.parity, :])\
                      .then_inc(d_row[r.parity], 16)
            turns(sp, turn)

            for par in range(2):
                sp.wait_ge(d_slot[par], 16 * 8 * NB // 2)
                sp.wait_ge(d_row[par], 16 * NB // 2)
                sp.wait_ge(d_x2[par], 16 * NB // 2)
            sp.dma_start(slot_table[:, :], table.rearrange("(p n) o -> p (n o)", p=HS)).then_inc(s_table, 16)

            def expert_turn(b):
                e = b["gather"]
                if e.exists():
                    wait(sp, gup_t, e.back(2), "second")
                    sp.dma_start(gu_sb[:, e.parity, :, :], gate_up[bass.ds(e.index * P, P), :, :])\
                      .then_inc(d_gu[e.parity], 16)
                    wait(sp, dwn_t, e.back(2), "y1")
                    sp.dma_start(dn_sb[:, e.parity, :], down_proj[bass.ds(e.index * INTER, P), :])\
                      .then_inc(d_dn[e.parity], 16)
                    sp.dma_start(dn2_sb[:, e.parity, :],
                                 down_proj[bass.ds(e.index * INTER + P, INTER - P), :])\
                      .then_inc(d_dn[e.parity], 16)
            expert_turns(sp, expert_turn)
            for par in range(2):
                sp.wait_ge(d_add[par], 16 * 2 * E // 2)

        @block.gpsimd
        def _(pool):
            pool.memset(ident[:, :], 0.0).then_inc(s_blank, 1)
            pool.memset(ones[:, :], 1.0)
            pool.memset(before_bf[:, :], 1.0).then_inc(s_blank, 1)
            pool.memset(neg_half[:, :], -0.5)
            pool.memset(zeros[:, :], 0.0)
            pool.iota(token_ids[:, :], [[P, NB]], base=0, channel_multiplier=1)
            pool.iota(spare_ids[:, :, :], [[0, E], [HS, 2]], base=T, channel_multiplier=1)
            pool.iota(expert_iota[:, :], [[1, E]], base=0, channel_multiplier=0,
                      allow_small_or_imprecise_dtypes=True)
            pool.iota(slot_base[:, :], [[2, E]], base=1, channel_multiplier=0,
                      allow_small_or_imprecise_dtypes=True)
            pool.memset(ones_bf[:, :], 1.0)
            pool.wait_ge(s_blank, 2)
            pool.affine_select(out=ident[:, :], in_=ident[:, :], compare_op=ALU.not_equal, fill=1.0, base=0,
                               pattern=[[-1, P]], channel_multiplier=1)
            pool.affine_select(out=before_bf[:, :], in_=before_bf[:, :], compare_op=ALU.is_gt, fill=0.0,
                               base=0, pattern=[[1, P]], channel_multiplier=-1).then_inc(s_made, 1)
            pool.wait_ge(s_made, 1)
            pool.dma_start(table.rearrange("(p n) o -> p (n o)", p=HS),
                           spare_ids[:, :, :].rearrange("p e h -> p (e h)")).then_inc(s_spare, 16)
            pool.dma_start(xw[T:T + CAP, :].rearrange("(p a) n -> p (a n)", a=2), zeros[:, :])\
                .then_inc(s_spare, 16)
            pool.dma_start(out[T:T + CAP, :].rearrange("(p a) n -> p (a n)", a=2), zeros[:, 0:2 * DM])\
                .then_inc(s_spare, 16)
            pool.wait_ge(s_spare, 48)

            def turn(b):
                n, a, c, o = b["norm"], b["attend"], b["cross"], b["route"]
                if c.exists():
                    wait(pool, crs_v, c, "eps")
                    pool.tensor_tensor(rstd2[:, :], mv2[:, 1:2], neg_half[:, 0:1], ALU.pow)\
                        .then_inc(crs_p.sem, 1)
                if o.exists():
                    wait(pool, out_v, o, "eps")
                    pool.tensor_tensor(rstd3[:, :], mv3[:, 1:2], neg_half[:, 0:1], ALU.pow)\
                        .then_inc(out_p.sem, 1)
                if a.exists():
                    wait(pool, att_v, a, "sqmean")
                    pool.tensor_tensor(rstd_h[:, :], sq_mean[:, :], neg_half[:, :], ALU.pow)\
                        .then_inc(att_p.sem, 1)
                if n.exists():
                    wait(pool, ln1, n, "eps")
                    pool.tensor_tensor(rstd1[:, :], mv1[:, 1:2], neg_half[:, 0:1], ALU.pow)\
                        .then_inc(ln1_p.sem, 1)
                if o.exists():
                    wait(pool, rte_v, o, "token")
                    settled(pool)
                    for k in range(8):
                        pool.indirect_dma_start(
                            out=table, out_offset=bass.IndirectOffsetOnAxis(ap=slot_idx[:, o.parity, k:k + 1], axis=0),
                            in_=token_id[:, o.parity:o.parity + 1], in_offset=None,
                            bounds_check=SLOTS - 1, oob_is_err=False).then_inc(d_slot[o.parity], 16)
            turns(pool, turn)

            def gather(e):
                wait(pool, ffn_v, e, "index")
                wait(pool, ffn_t, e.back(2), "rowsT1")
                wait(pool, ffn_v, e.back(2), "weight")
                settled(pool)
                for h in range(2):
                    pool.indirect_dma_start(
                        out=rows[:, e.parity, h, :], out_offset=None, in_=xw,
                        in_offset=bass.IndirectOffsetOnAxis(ap=gather_idx[:, e.parity, h:h + 1], axis=0),
                        bounds_check=T + CAP - 1, oob_is_err=True).then_inc(d_rows[e.parity], 16)

            def expert_turn(b):
                g, d = b["gather"], b["down"]
                if g.exists():
                    gather(g)
                if d.exists():
                    wait_dma(pool, d_add, d.back(1), 2)
                    wait(pool, dwn_a, d, "y0")
                    wait(pool, dwn_v, d, "y1")
                    settled(pool)
                    for h in range(2):
                        pool.indirect_dma_start(
                            out=out, out_offset=bass.IndirectOffsetOnAxis(ap=scatter_idx[:, d.parity, h:h + 1], axis=0),
                            in_=y[:, d.parity, h, :], in_offset=None,
                            bounds_check=T + CAP - 1, oob_is_err=True,
                            compute_op=ALU.add).then_inc(d_add[d.parity], 16)
            expert_turns(pool, expert_turn)

        @block.scalar
        def _(act):
            for n in range(4):
                act.dma_start(lam_in[:, n, :], lambdas[n].partition_broadcast(P)).then_inc(s_late, 16)
            act.dma_start(subln_sb[:, :], subln.rearrange("(p o) -> p o", o=1)).then_inc(s_late, 16)
            act.dma_start(o2n_i[:, :], old_to_new.rearrange("(p o) -> p o", o=1)).then_inc(s_late, 16)
            act.dma_start(gate_sb[:, :], gate).then_inc(s_late, 16)
            act.dma_start(mask_sb[:, :], mask.partition_broadcast(P)).then_inc(s_late, 16)
            act.dma_start(wout_sb[:, :, :], wout).then_inc(s_late, 16)
            act.wait_ge(s_setup_v, 2)
            act.activation(lam_exp[:, :], lam_sum[:, :], ACT.Exp).then_inc(s_setup_act, 1)

            def copy(dst, src, steps, scale=None):
                if scale is None:
                    act.activation(dst, src, ACT.Copy).then_inc(steps.sem, 1)
                else:
                    act.activation(dst, src, ACT.Copy, scale=scale).then_inc(steps.sem, 1)

            def turn(b):
                p, a, c, r = b["project"], b["attend"], b["cross"], b["route"]
                if a.exists():
                    wait(act, att_v, a, "negmax")
                    wait(act, att_v, a.back(1), "weighted")
                    for s in range(2):
                        for h in range(H):
                            last = act.activation(probs[:, s, h, :], blocks(banks_s[:, s, :])[:, h, :], ACT.Exp,
                                                  bias=neg_max_s[:, s, h:h + 1], scale=INV_SCALING,
                                                  accum_out=prob_sum[:, s, h:h + 1])
                    last.then_inc(att_a.sem, 1)
                if p.exists():
                    wait(act, prj_t, p, "xT")
                    wait(act, prj_t, p.back(1), "v")
                    copy(xn1_t[:, :, :], blocks(bank_ta), prj_a)
                if c.exists():
                    wait(act, crs_t, c, "xT")
                    copy(xn2_t[:, :, :], blocks(bank_tb), crs_a)
                if r.exists():
                    wait(act, rte_t, r, "xT")
                    copy(xn3_t[:, :, :], blocks(bank_ta), rte_a)
                if c.exists():
                    wait(act, crs_v, c, "shifted")
                    wait(act, out_v, c.back(1), "inv")
                    act.activation(xprobs[:, :], xshifted[:, :], ACT.Exp, scale=XSCALE,
                                   accum_out=xsum[:, :]).then_inc(crs_a.sem, 1)
                if r.exists():
                    wait(act, rte_v, r, "negmax")
                    act.activation(lexp[:, :], logits[:, :], ACT.Exp, bias=lneg_max[:, :])\
                        .then_inc(rte_a.sem, 1)
                if a.exists():
                    wait(act, att_t, a, "diffT")
                    copy(diff_t[:, :, :], blocks(bank_tb), att_a)
                if p.exists():
                    wait(act, prj_t, p, "v")
                    wait(act, att_t, p.back(2), "pv")
                    copy(v_sb[:, p.parity, :], bank_v, prj_a)
                if c.exists():
                    wait(act, crs_t, c, "probsT")
                    copy(xprobs_t[:, :], bank_ta[:, 0:P], crs_a)
                if a.exists():
                    wait(act, att_t, a, "pv")
                    act.activation(squares[:, :, :], blocks(bank_o), ACT.Square).then_inc(att_a.sem, 1)
                if p.exists():
                    wait(act, prj_t, p, "qT")
                    wait(act, att_t, p.back(1), "scores")
                    copy(q_t[:, :, :], blocks(bank_tb), prj_a)
                    wait(act, prj_t, p, "kT")
                    copy(k_t[:, :, :], blocks(bank_ta), prj_a)
                if a.exists():
                    wait(act, att_t, a, "headsT")
                    wait(act, att_t, a.back(1), "proj")
                    copy(heads_t[:, :, :], blocks(bank_tb), att_a, scale=subln_sb[:, :])
            act.wait_ge(s_late, 16 * 9)
            turns(act, turn)

            def expert_turn(b):
                g, u, d = b["gather"], b["up"], b["down"]
                if g.exists():
                    wait(act, ffn_t, g, "rowsT0")
                    wait(act, gup_t, g.back(2), "second")
                    copy(rows_t[:, g.parity, :, 0:HS], ps[:, 0, 0:KC * HS].rearrange("p (c n) -> p c n", c=KC),
                         ffn_a)
                if u.exists():
                    wait(act, gup_t, u, "first")
                    wait(act, gup_v, u.back(1), "h2")
                    act.activation(silu1[:, :], ps[:, 2, 0:CAP], ACT.Silu).then_inc(gup_a.sem, 1)
                    wait(act, gup_t, u, "second")
                    act.activation(silu2[:, :], ps[0:INTER - P, 3, 0:CAP], ACT.Silu).then_inc(gup_a.sem, 1)
                if d.exists():
                    wait(act, dwn_t, d, "y0")
                    wait(act, ffn_v, d, "weight")
                    wait_dma(act, d_add, d.back(2), 2)
                    copy(y[:, d.parity, 0, :], ps[0:HS, 4, :], dwn_a, scale=weight_of[d.parity][:, 0:1])
            expert_turns(act, expert_turn)

        @block.vector
        def _(dve):
            dve.wait_ge(s_late, 16 * 9)
            dve.tensor_tensor(lam_prod[:, :, :], lam_in[:, 0:2, :], lam_in[:, 2:4, :], ALU.mult)\
                .then_inc(s_setup_v, 1)
            dve.wait_ge(s_setup_v, 1)
            dve.reduce_sum(lam_sum[:, :], lam_prod[:, :, :], AX.X).then_inc(s_setup_v, 1)
            dve.tensor_copy(o2n_f[:, :], o2n_i[:, :]).then_inc(s_setup_v, 1)
            dve.reduce_max(valid[:, :], mask_sb[:, :].rearrange("p (b m) -> p b m", m=M), AX.X)\
                .then_inc(s_setup_v, 1)
            dve.memset(taken[:, :], 0.0)
            dve.wait_ge(s_setup_v, 4)
            dve.wait_ge(s_made, 1)
            dve.tensor_scalar(is_new[:, :], expert_iota[:, :], o2n_f[:, :], None, ALU.is_equal)\
                .then_inc(s_setup_v, 1)
            dve.wait_ge(s_setup_act, 1)
            dve.tensor_tensor(lam_gap[:, :], lam_exp[:, 1:2], lam_exp[:, 0:1], ALU.subtract)\
                .then_inc(s_setup_v, 1)
            dve.wait_ge(s_setup_v, 6)
            dve.tensor_scalar_add(neg_lam[:, :], lam_gap[:, :], -LAMBDA_INIT).then_inc(s_setup_v, 1)
            dve.wait_ge(s_setup_pe, 1)
            dve.tensor_copy(gate_new[:, :, :], ps[:, 0, 0:KC * E].rearrange("p (c e) -> p c e", c=KC))\
                .then_inc(s_setup_v, 1)
            dve.tensor_scalar(absent_bias[:, :], ps[:, 1, 0:E], -1.0, BIG, ALU.add, ALU.mult)\
                .then_inc(s_setup_v, 1)
            dve.wait_ge(s_setup_v, 9)

            def step(steps, ins):
                ins.then_inc(steps.sem, 1)

            def norm_stats(steps, b, src, st, mv):
                step(steps, dve.bn_stats(st[:, :], src))
                wait(dve, steps, b, "stats")
                settled(dve)
                step(steps, dve.bn_aggr(mv[:, :], st[:, :]))
                wait(dve, steps, b, "aggr")
                step(steps, dve.tensor_scalar_add(mv[:, 1:2], mv[:, 1:2], EPS))

            def turn(b):
                n, p, a, c, r = (b[k] for k in ("norm", "project", "attend", "cross", "route"))
                if a.exists():
                    wait(dve, att_t, a, "scores")
                    wait(dve, att_a, a.back(1), "exp")
                    step(att_v, dve.tensor_reduce(neg_max[:, :, :], banks_s.rearrange("p s (h n) -> p s h n", n=P),
                                                  AX.X, ALU.max, negate=True))
                    wait(dve, att_v, a, "max")
                    step(att_v, dve.tensor_scalar_mul(neg_max_s[:, :, :], neg_max[:, :, :], INV_SCALING))
                if c.exists():
                    wait_dma(dve, d_xres, c, 1)
                    wait(dve, att_t, c, "proj")
                    step(crs_v, dve.tensor_tensor(x1[:, c.parity, :], bank_o, x_res[:, c.parity, :], ALU.add))
                    wait(dve, crs_v, c, "x1")
                    norm_stats(crs_v, c, x1[:, c.parity, :], st2, mv2)
                if r.exists():
                    wait(dve, crs_a, r, "exp")
                    step(out_v, dve.reciprocal(xinv[:, :], xsum[:, :]))
                    wait(dve, out_v, r, "inv")
                    settled(dve)
                    step(out_v, dve.tensor_scalar(xcoef[:, :], valid[:, bass.ds(r.index, 1)], xinv[:, :], None,
                                                  ALU.mult))
                    wait(dve, out_v, r, "coef")
                    wait(dve, crs_t, r, "readout")
                    wait_dma(dve, d_x2, r.back(2), 1)
                    step(out_v, dve.scalar_tensor_tensor(x2[:, r.parity, :], bank_v, xcoef[:, :], x1[:, r.parity, :],
                                                         ALU.mult, ALU.add))
                    wait(dve, out_v, r, "x2")
                    norm_stats(out_v, r, x2[:, r.parity, :], st3, mv3)
                if c.exists():
                    wait(dve, crs_p, c, "rstd")
                    wait(dve, crs_t, c.back(1), "xT")
                    step(crs_v, dve.tensor_scalar(xn2[:, :], x1[:, c.parity, :], mv2[:, 0:1], rstd2[:, :],
                                                  ALU.subtract, ALU.mult))
                if r.exists():
                    wait(dve, out_p, r, "rstd")
                    wait_dma(dve, d_row, r.back(2), 1)
                    step(out_v, dve.tensor_scalar(row[:, r.parity, 0:DM], x2[:, r.parity, :], mv3[:, 0:1], rstd3[:, :],
                                                  ALU.subtract, ALU.mult))
                if c.exists():
                    mask_row = mask_sb[:, bass.ds(c.index * M, M)]
                    wait(dve, crs_v, c.back(1), "score")
                    settled(dve)
                    step(crs_v, dve.tensor_scalar(mask_bias[:, :], mask_row, -1.0, BIG, ALU.add, ALU.mult))
                    wait(dve, crs_t, c, "scores")
                    settled(dve)
                    step(crs_v, dve.tensor_tensor(xscore_kept[:, :], bank_o[:, 0:M], mask_row, ALU.mult))
                    wait(dve, crs_v, c, "kept")
                    step(crs_v, dve.tensor_tensor(xscore[:, :], xscore_kept[:, :], mask_bias[:, :], ALU.add))
                    wait(dve, crs_v, c, "score")
                    step(crs_v, dve.tensor_reduce(xneg_max[:, :], xscore[:, :], AX.X, ALU.max, negate=True))
                    wait(dve, crs_v, c, "max")
                    wait(dve, crs_a, c.back(1), "exp")
                    step(crs_v, dve.tensor_scalar(xshifted[:, :], xscore[:, :], xneg_max[:, :], None, ALU.add))
                if r.exists():
                    wait(dve, rte_t, r, "logits")
                    wait(dve, rte_a, r.back(1), "exp")
                    step(rte_v, dve.tensor_tensor(logits[:, :], bank_v[:, 0:E], absent_bias[:, :], ALU.add))
                    wait(dve, rte_v, r, "logits")
                    settled(dve)
                    step(rte_v, dve.max(top8[:, :], logits[:, :]))
                    wait(dve, rte_v, r, "top8")
                    settled(dve)
                    step(rte_v, dve.match_replace(rest[:, :], top8[:, :], logits[:, :], -3e38))
                    wait(dve, rte_v, r, "rest")
                    step(rte_v, dve.tensor_tensor(chosen[:, :], rest[:, :], logits[:, :], ALU.is_lt))
                    step(rte_v, dve.tensor_scalar_mul(lneg_max[:, :], top8[:, 0:1], -1.0))
                if a.exists():
                    wait(dve, att_a, a, "exp")
                    step(att_v, dve.reciprocal(coef[:, :, :], prob_sum[:, :, :]))
                    wait(dve, att_v, a, "inv")
                    step(att_v, dve.tensor_scalar(coef[:, 1, :], coef[:, 1, :], neg_lam[:, :], None, ALU.mult))
                    wait(dve, att_v, a, "coef")
                    step(att_v, dve.tensor_tensor(
                        weighted[:, :, :, :].rearrange("p s h n -> p (s h) n"),
                        probs[:, :, :, :].rearrange("p s h n -> p (s h) n"),
                        coef[:, :, :].rearrange("p s h -> p (s h)").unsqueeze(2).to_broadcast([P, 2 * H, P]),
                        ALU.mult))
                    wait(dve, att_v, a, "weighted")
                    wait(dve, att_t, a.back(1), "diffT")
                    step(att_v, dve.tensor_tensor(diff[:, :, :], weighted[:, 0, :, :], weighted[:, 1, :, :], ALU.add))
                if p.exists():
                    qk = banks_qk.rearrange("p a (g f) -> p (a g) f", f=NF)
                    wait(dve, prj_t, p, "qk")
                    for name, buf, i in (("cos", qk_cos, 0), ("sin", qk_sin, 1)):
                        step(rope, dve.tensor_tensor(
                            buf[:, :, :, :].rearrange("p g r f -> p (g r) f"), qk,
                            rope_tab[:, i:i + 1, :].to_broadcast([P, 4 * NH2, NF]), ALU.mult))
                    wait(dve, rope, p, "sin")
                    wait(dve, prj_t, p.back(1), "kT")
                    step(rope, dve.tensor_tensor(qk_rot[:, :, 0, :], qk_cos[:, :, 0, :], qk_sin[:, :, 1, :],
                                                 ALU.subtract))
                    step(rope, dve.tensor_tensor(qk_rot[:, :, 1, :], qk_cos[:, :, 1, :], qk_sin[:, :, 0, :], ALU.add))
                if a.exists():
                    wait(dve, att_a, a, "square")
                    step(att_v, dve.reduce_sum(sq_sum[:, :], squares[:, :, :], AX.X))
                    wait(dve, att_v, a, "sqsum")
                    step(att_v, dve.tensor_scalar(sq_mean[:, :], sq_sum[:, :], 1.0 / P, EPS, ALU.mult, ALU.add))
                    wait(dve, att_p, a, "rstd")
                    wait(dve, att_t, a.back(1), "headsT")
                    step(att_v, dve.tensor_tensor(heads[:, :, :], blocks(bank_o),
                                                  rstd_h[:, :].unsqueeze(2).to_broadcast([P, H, P]), ALU.mult))
                if r.exists():
                    wait(dve, rte_a, r, "exp")
                    step(rte_v, dve.scalar_tensor_tensor(lexp_chosen[:, :], lexp[:, :], 1.0, chosen[:, :],
                                                         ALU.mult, ALU.mult, accum_out=wsum[:, :]))
                    wait(dve, rte_v, r, "wsum")
                    step(rte_v, dve.reciprocal(winv[:, :], wsum[:, :]))
                    wait(dve, rte_v, r, "winv")
                    step(rte_v, dve.tensor_scalar(row[:, r.parity, DM:ROW], lexp_chosen[:, :], winv[:, :], None,
                                                  ALU.mult))
                    counts = banks_qk[:, 0, :]
                    wait(dve, rte_t, r, "counts")
                    step(rte_v, dve.tensor_tensor(pos[:, :], counts[:, 0:E], taken[:, :], ALU.add))
                    wait(dve, rte_v, r, "pos")
                    step(rte_v, dve.scalar_tensor_tensor(fits[:, :], pos[:, :], float(CAP), chosen[:, :],
                                                         ALU.is_lt, ALU.mult))
                    step(rte_v, dve.tensor_scalar(second_half[:, :], pos[:, :], float(HS), float(1 - 2 * E * HS),
                                                  ALU.is_ge, ALU.mult))
                    step(rte_v, dve.scalar_tensor_tensor(address[:, :], pos[:, :], float(2 * E), slot_base[:, :],
                                                         ALU.mult, ALU.add))
                    wait(dve, rte_v, r, "addr")
                    step(rte_v, dve.tensor_tensor(address2[:, :], address[:, :], second_half[:, :], ALU.add))
                    step(rte_v, dve.tensor_tensor(taken[:, :], counts[:, E:2 * E], taken[:, :], ALU.add))
                    wait(dve, rte_v, r, "addr2")
                    step(rte_v, dve.tensor_tensor(key[:, :], address2[:, :], fits[:, :], ALU.mult))
                    wait(dve, rte_v, r, "key")
                    settled(dve)
                    step(rte_v, dve.max(slot8[:, :], key[:, :]))
                    wait(dve, rte_v, r, "slot8")
                    step(rte_v, dve.tensor_scalar(no_slot[:, :], slot8[:, :], 0.0, 1e6, ALU.is_equal, ALU.mult))
                    wait(dve, rte_v, r, "none")
                    wait_dma(dve, d_slot, r.back(2), 8)
                    step(rte_v, dve.scalar_tensor_tensor(slot_idx[:, r.parity, :], no_slot[:, :], -1.0, slot8[:, :],
                                                         ALU.add, ALU.add))
                    settled(dve)
                    step(rte_v, dve.tensor_copy(token_id[:, r.parity:r.parity + 1], token_ids[:, bass.ds(r.index, 1)]))
                if n.exists():
                    wait_dma(dve, d_xln, n, 1)
                    norm_stats(ln1, n, x_ln[:, n.parity, :], st1, mv1)
                    wait(dve, ln1_p, n, "rstd")
                    wait(dve, prj_t, n.back(2), "xT")
                    step(ln1, dve.tensor_scalar(xn1[:, n.parity, :], x_ln[:, n.parity, :], mv1[:, 0:1], rstd1[:, :],
                                                ALU.subtract, ALU.mult))
            turns(dve, turn)

            dve.wait_ge(s_table, 16)

            def expert_turn(b):
                g, u, d = b["gather"], b["up"], b["down"]
                if g.exists():
                    wait_dma(dve, d_rows, g.back(2), 2)
                    settled(dve)
                    step(ffn_v, dve.tensor_copy(gather_idx[:, g.parity, :], slot_table[:, bass.ds(2 * g.index, 2)]))
                if d.exists():
                    wait_dma(dve, d_add, d.back(2), 2)
                    settled(dve)
                    step(dwn_v, dve.tensor_copy(scatter_idx[:, d.parity, :], slot_table[:, bass.ds(2 * d.index, 2)]))
                if u.exists():
                    wait(dve, gup_a, u, "silu1")
                    wait(dve, dwn_t, u.back(2), "y1")
                    step(gup_v, dve.tensor_tensor(h1[:, u.parity, :], silu1[:, :], ps[:, 2, CAP:2 * CAP], ALU.mult))
                    wait(dve, gup_a, u, "silu2")
                    step(gup_v, dve.tensor_tensor(h2[:, u.parity, :], silu2[:, :], ps[INTER - P:P, 3, 0:CAP], ALU.mult))
                if d.exists():
                    wait(dve, dwn_t, d, "y1")
                    step(dwn_v, dve.tensor_scalar(y[:, d.parity, 1, :], ps[0:HS, 5, :], weight_of[d.parity][:, 1:2], None,
                                                  ALU.mult))
                if g.exists():
                    wait_dma(dve, d_rows, g, 2)
                    wait(dve, dwn_a, g.back(2), "y0")
                    wait(dve, dwn_v, g.back(2), "y1")
                    settled(dve)
                    step(ffn_v, dve.tensor_copy(weight_of[g.parity][:, :], rows[:, g.parity, :, bass.ds(g.index + DM, 1)]
                                                .rearrange("p h o -> p (h o)")))
                    wait(dve, ffn_t, g, "rowsT1")
                    wait(dve, gup_t, g.back(2), "second")
                    step(ffn_v, dve.tensor_copy(rows_t[:, g.parity, :, HS:CAP],
                                                ps[:, 1, 0:KC * HS].rearrange("p (c n) -> p c n", c=KC)))
            expert_turns(dve, expert_turn)

        @block.tensor
        def _(pe):
            pe.wait_ge(s_setup_v, 5)
            for c in range(KC):
                pe.matmul(ps[:, 0, c * E:(c + 1) * E], gate_sb[:, c * P:(c + 1) * P], is_new[:, :],
                          start=True, stop=True)
            pe.matmul(ps[:, 1, 0:E], ones[:, :], is_new[:, :], start=True, stop=True).then_inc(s_setup_pe, 1)
            pe.wait_ge(s_setup_v, 9)
            pe.wait_ge(s_weights, 48)

            def step(steps, ins):
                ins.then_inc(steps.sem, 1)

            def transpose4(bank, src):
                for c in range(KC):
                    last = pe.transpose(blocks(bank)[:, c, :], src(c), ident[:, :])
                return last

            def product(dst, left, right, n=KC):
                for c in range(n):
                    last = pe.matmul(dst, left(c), right(c), start=(c == 0), stop=(c == n - 1))
                return last

            def turn(b):
                p, a, c, r = b["project"], b["attend"], b["cross"], b["route"]
                if a.exists():
                    wait(pe, prj_a, a, "kT")
                    wait(pe, att_a, a.back(1), "exp")
                    for h in range(H):
                        for s in range(2):
                            half = slice(s * HALF, (s + 1) * HALF)
                            last = pe.matmul(blocks(banks_s[:, s, :])[:, h, :], q_t[half, h, :], k_t[half, h, :],
                                             start=True, stop=True)
                    step(att_t, last)
                if p.exists():
                    wait(pe, ln1, p, "normed")
                    wait(pe, prj_a, p.back(1), "kT")
                    step(prj_t, transpose4(bank_ta, lambda k: xn1[:, p.parity, k * P:(k + 1) * P]))
                    wait(pe, prj_a, p, "xT")
                    wait(pe, rte_v, r.back(1), "taken")
                    product(banks_qk[:, 0, :], lambda k: xn1_t[:, k, :], lambda k: wqk_sb[:, k, 0:DM])
                if c.exists():
                    wait(pe, crs_v, c, "normed")
                    wait(pe, att_a, a.back(1), "headsT")
                    step(crs_t, transpose4(bank_tb, lambda k: xn2[:, k * P:(k + 1) * P]))
                if r.exists():
                    wait(pe, out_v, r, "normed")
                    wait(pe, prj_a, p, "xT")
                    step(rte_t, transpose4(bank_ta, lambda k: row[:, r.parity, k * P:(k + 1) * P]))
                if p.exists():
                    step(prj_t, product(banks_qk[:, 1, :], lambda k: xn1_t[:, k, :], lambda k: wqk_sb[:, k, DM:2 * DM]))
                if c.exists():
                    wait(pe, crs_a, c, "xT")
                    wait_dma(pe, d_ctx, c, 2)
                    step(crs_t, product(bank_o[:, 0:M], lambda k: xn2_t[:, k, :], lambda k: ctx_t_sb[:, c.parity, k, :]))
                if r.exists():
                    wait(pe, rte_a, r, "xT")
                    step(rte_t, product(bank_v[:, 0:E], lambda k: xn3_t[:, k, :], lambda k: gate_new[:, k, :]))
                if a.exists():
                    wait(pe, att_v, a, "diff")
                    wait(pe, crs_a, c, "xT")
                    step(att_t, transpose4(bank_tb, lambda k: diff[:, k, :]))
                if p.exists():
                    wait(pe, rte_v, r, "logits")
                    step(prj_t, product(bank_v, lambda k: xn1_t[:, k, :], lambda k: wv_sb[:, k, :]))
                if c.exists():
                    wait(pe, crs_a, c, "exp")
                    wait(pe, rte_a, r, "xT")
                    step(crs_t, pe.transpose(bank_ta[:, 0:P], xprobs[:, :], ident[:, :]))
                if a.exists():
                    wait(pe, att_a, a, "diffT")
                    wait(pe, crs_v, c, "kept")
                    for h in range(H):
                        last = pe.matmul(blocks(bank_o)[:, h, :], diff_t[:, h, :],
                                         v_sb[:, a.parity, h * P:(h + 1) * P], start=True, stop=True)
                    step(att_t, last)
                if c.exists():
                    wait(pe, crs_a, c, "probsT")
                    wait(pe, prj_a, p, "v")
                    step(crs_t, pe.matmul(bank_v, xprobs_t[:, :], ctx_sb[:, c.parity, :], start=True, stop=True))
                if p.exists():
                    wait(pe, rope, p, "imag")
                    wait(pe, att_a, a, "diffT")
                    rot = qk_rot[:, :, :, :].rearrange("p g r f -> p (g r f)")
                    step(prj_t, transpose4(bank_tb, lambda k: rot[:, k * P:(k + 1) * P]))
                    wait(pe, crs_a, c, "probsT")
                    step(prj_t, transpose4(bank_ta, lambda k: rot[:, DM + k * P:DM + (k + 1) * P]))
                if r.exists():
                    wait(pe, rte_v, r, "chosen")
                    pe.matmul(banks_qk[:, 0, 0:E], before_bf[:, :], chosen[:, :], start=True, stop=True)
                    step(rte_t, pe.matmul(banks_qk[:, 0, E:2 * E], ones_bf[:, :], chosen[:, :], start=True, stop=True))
                if a.exists():
                    wait(pe, att_v, a, "heads")
                    wait(pe, prj_a, p, "qT")
                    step(att_t, transpose4(bank_tb, lambda k: heads[:, k, :]))
                    wait(pe, att_a, a, "headsT")
                    step(att_t, product(bank_o, lambda k: heads_t[:, k, :], lambda k: wout_sb[:, k, :]))
            turns(pe, turn)

            def expert_turn(b):
                g, u, d = b["gather"], b["up"], b["down"]
                if g.exists():
                    wait_dma(pe, d_rows, g, 2)
                    for h in range(2):
                        if h == 0:
                            wait(pe, ffn_a, g.back(1), "rowsT0")
                        else:
                            wait(pe, ffn_v, g.back(1), "rowsT1")
                        for c in range(KC):
                            last = pe.transpose(ps[:, h, c * HS:(c + 1) * HS], rows[:, g.parity, h, c * P:(c + 1) * P],
                                                ident[0:HS, 0:HS])
                        step(ffn_t, last)
                if u.exists():
                    wait_dma(pe, d_gu, u, 1)
                    wait(pe, ffn_a, u, "rowsT0")
                    wait(pe, ffn_v, u, "rowsT1")
                    wait(pe, gup_v, u.back(1), "h2")
                    for m in range(2):
                        last = product(ps[:, 2, m * CAP:(m + 1) * CAP],
                                       lambda k: gu_sb[:, u.parity, k, m * P:(m + 1) * P],
                                       lambda k: rows_t[:, u.parity, k, :])
                    step(gup_t, last)
                    step(gup_t, product(ps[:, 3, 0:CAP], lambda k: gu_sb[:, u.parity, k, 2 * P:3 * P],
                                        lambda k: rows_t[:, u.parity, k, :]))
                if d.exists():
                    wait_dma(pe, d_dn, d, 2)
                    wait(pe, gup_v, d, "h2")
                    for h in range(2):
                        if h == 0:
                            wait(pe, dwn_a, d.back(1), "y0")
                        else:
                            wait(pe, dwn_v, d.back(1), "y1")
                        half = slice(h * HS, (h + 1) * HS)
                        pe.matmul(ps[0:HS, 4 + h, :], h1[:, d.parity, half], dn_sb[:, d.parity, :],
                                  start=True, stop=False)
                        step(dwn_t, pe.matmul(ps[0:HS, 4 + h, :], h2[:, d.parity, half], dn2_sb[:, d.parity, :],
                                              start=False, stop=True))
            expert_turns(pe, expert_turn)


def kernel(x, ctx_2048, mask_BxS2_bk0, L0_attn_wq, L0_attn_wk, L0_attn_wv, L0_attn_wout, L0_attn_lambda_q1,
           L0_attn_lambda_q2, L0_attn_lambda_k1, L0_attn_lambda_k2, L0_attn_subln_weight, L0_ffn_gate_weight,
           L0_ffn_gate_up_proj, L0_ffn_down_proj, L0_ffn_old_to_new):
    import concourse.bacc as bacc
    from concourse.bass_utils import run_bass_kernel_spmd

    f = lambda a: np.ascontiguousarray(np.asarray(a))

    def chunked(w):
        return w.T.reshape(w.shape[1] // P, P, w.shape[0]).transpose(1, 0, 2)

    def halves(w):
        return w.reshape(NH2, NF, 2, DM).transpose(0, 2, 1, 3).reshape(DM, DM)

    wq, wk = halves(f(L0_attn_wq)), halves(f(L0_attn_wk))
    gu = f(L0_ffn_gate_up_proj)
    g, u = gu[:, :INTER], gu[:, INTER:]
    gu = np.concatenate([g[:, :P], u[:, :P], g[:, P:], u[:, P:]], axis=1)
    gu = gu.transpose(0, 2, 1).reshape(E, KC, P, 2 * INTER).transpose(0, 2, 1, 3).reshape(E * P, KC, 2 * INTER)
    ctx = f(ctx_2048)
    angle = np.outer(np.arange(P), 1.0 / 10000.0 ** (np.arange(0, HALF, 2).astype(np.float64) / HALF))
    arrays = {
        "x": f(x).reshape(T, DM),
        "ctx_rows": ctx.reshape(NB * M, DM),
        "ctx_t": ctx.transpose(0, 2, 1).reshape(NB, KC, P, M).transpose(0, 2, 1, 3).reshape(NB * P, KC, M),
        "mask": f(mask_BxS2_bk0).reshape(NB * M),
        "wqk": chunked(np.concatenate([wq, wk], axis=0)),
        "wv": chunked(f(L0_attn_wv)),
        "wout": chunked(f(L0_attn_wout)),
        "lambda_q1": f(L0_attn_lambda_q1),
        "lambda_q2": f(L0_attn_lambda_q2),
        "lambda_k1": f(L0_attn_lambda_k1),
        "lambda_k2": f(L0_attn_lambda_k2),
        "subln": f(L0_attn_subln_weight),
        "gate": f(L0_ffn_gate_weight),
        "gate_up": gu,
        "down_proj": f(L0_ffn_down_proj).transpose(0, 2, 1).reshape(E * INTER, DM),
        "old_to_new": f(L0_ffn_old_to_new),
        "cos_sin": np.stack([np.cos(angle), np.sin(angle)], axis=1).astype(np.float32),
    }
    arrays = {k: np.ascontiguousarray(v) for k, v in arrays.items()}
    nc = bacc.Bacc("TRN2", target_bir_lowering=False, num_devices=1)
    ap = {k: nc.dram_tensor(f"in_{k}", v.shape, mybir.dt.from_np(v.dtype), kind="ExternalInput").ap()
          for k, v in arrays.items()}
    out = nc.dram_tensor("layer_out", (T + CAP, DM), FP32, kind="ExternalOutput").ap()
    lambdas = [ap.pop(k) for k in ("lambda_q1", "lambda_q2", "lambda_k1", "lambda_k2")]
    decoder_layer(nc, lambdas=lambdas, out=out, **ap)
    result = run_bass_kernel_spmd(nc, [{f"in_{k}": v for k, v in arrays.items()}], core_ids=[0])
    return np.asarray(result.results[0]["layer_out"])[:T].reshape(NB, P, DM)
```

```python
import math
from contextlib import ExitStack

import numpy as np

import concourse.bass as bass
from concourse import mybir

FP32 = mybir.dt.float32
FP32R = mybir.dt.float32r
BF16 = mybir.dt.bfloat16
I32 = mybir.dt.int32
U8 = mybir.dt.uint8
ALU = mybir.AluOpType
ACT = mybir.ActivationFunctionType
AX = mybir.AxisListType

P = 128
NB = 32
DM = 512
KC = DM // P
NH2 = 8
HALF = 64
NF = HALF // 2
H = NH2 // 2
M = 128
NEXP = 128
E = 48
INTER = 192
CAP = 192
HS = CAP // 2
T = NB * P
EPS = 1e-5
INV_SCALING = float(P) ** 0.5
XSCALE = float(DM) ** -0.5
LAMBDA_INIT = 0.8 - 0.6 * math.exp(-0.3 * 12)
BIG = 1e30
ROW = DM + E
SLOTS = HS * 2 * E


class Batch:

    def __init__(self, pair, off, limit):
        self.pair, self.off, self.limit = pair, off, limit
        self.parity = off % 2
        self.half = pair + off // 2
        self.index = 2 * pair + off

    def exists(self):
        return not isinstance(self.pair, int) or 0 <= self.index < self.limit

    def back(self, n):
        return Batch(self.pair, self.off - n, self.limit)


class Steps:

    def __init__(self, sem, names):
        self.sem, self.names = sem, names.split()

    def after(self, b, name):
        return len(self.names) * b.index + self.names.index(name) + 1


def wait(eng, steps, b, name):
    if b.exists():
        eng.wait_ge(steps.sem, steps.after(b, name))


def wait_dma(eng, sems, b, per_batch):
    if b.exists():
        eng.wait_ge(sems[b.parity], b.half * (16 * per_batch) + 16 * per_batch)


def decoder_layer(nc, x, ctx_rows, ctx_t, mask, weights, lambdas, subln, gate, gate_up, down_proj,
                  old_to_new, cos_sin, out):
    xw = nc.dram_tensor("normed_rows_and_weights", (T + CAP, ROW), FP32, kind="Internal").ap()
    table = nc.dram_tensor("token_of_slot", (SLOTS, 1), I32, kind="Internal").ap()

    stack = ExitStack()
    with stack:
        def sb(name, shape, dt=FP32):
            return stack.enter_context(nc.sbuf_tensor(name, shape, dt))

        def sem(name):
            return stack.enter_context(nc.semaphore(name))

        w_raw = sb("w_raw", [P, 2, KC, DM])
        w_high = sb("w_high", [P, 4, KC, DM], FP32R)
        w_low = sb("w_low", [P, 4, KC, DM], FP32R)
        W_Q, W_K, W_V, W_OUT = range(4)
        gate_sb = sb("gate_sb", [NEXP, DM])
        gate_new = sb("gate_new", [P, KC, E])
        rope_tab = sb("rope_tab", [P, 2, NF])
        lam_in = sb("lam_in", [P, 4, HALF])
        lam_prod = sb("lam_prod", [P, 2, HALF])
        lam_sum = sb("lam_sum", [P, 2])
        lam_exp = sb("lam_exp", [P, 2])
        lam_gap = sb("lam_gap", [P, 1])
        neg_lam = sb("neg_lam", [P, 1])
        subln_sb = sb("subln_sb", [P, 1])
        mask_sb = sb("mask_sb", [P, NB * M], U8)
        valid = sb("valid", [P, NB])
        ident = sb("ident", [P, P])
        ones = sb("ones", [P, P])
        ones_bf = sb("ones_bf", [P, P], BF16)
        before_bf = sb("before_bf", [P, P], BF16)
        neg_half = sb("neg_half", [P, H])
        o2n_i = sb("o2n_i", [NEXP, 1], I32)
        o2n_f = sb("o2n_f", [NEXP, 1])
        expert_iota = sb("expert_iota", [P, E])
        is_new = sb("is_new", [NEXP, E])
        absent_bias = sb("absent_bias", [P, E])
        slot_base = sb("slot_base", [P, E])
        token_ids = sb("token_ids", [P, NB], I32)
        spare_ids = sb("spare_ids", [HS, E, 2], I32)

        x_ln = sb("x_ln", [P, 2, DM])
        qk_both = sb("qk_both", [P, 4 * DM])
        zeros = qk_both[0:HS, 0:2 * ROW]
        st1 = sb("st1", [P, 6])
        mv1 = sb("mv1", [P, 2])
        rstd1 = sb("rstd1", [P, 1])
        xn1 = sb("xn1", [P, 2, DM])
        xn1_high = sb("xn1_high", [P, KC, P], FP32R)
        xn1_low = sb("xn1_low", [P, KC, P], FP32R)
        qk_cos = qk_both[:, 0:2 * DM].rearrange("p (g r f) -> p g r f", r=2, f=NF)
        qk_sin = qk_both[:, 2 * DM:4 * DM].rearrange("p (g r f) -> p g r f", r=2, f=NF)
        qk_rot = sb("qk_rot", [P, 2 * NH2, 2, NF])
        q_t = sb("q_t", [P, H, P])
        k_t = sb("k_t", [P, H, P])
        v_sb = sb("v_sb", [P, 2, DM])
        neg_max = sb("neg_max", [P, 2, H])
        neg_max_s = sb("neg_max_s", [P, 2, H])
        probs = sb("probs", [P, 2, H, P])
        prob_sum = sb("prob_sum", [P, 2, H])
        coef = sb("coef", [P, 2, H])
        weighted = sb("weighted", [P, 2, H, P])
        diff = sb("diff", [P, H, P])
        diff_t = sb("diff_t", [P, H, P])
        squares = sb("squares", [P, H, P])
        sq_sum = sb("sq_sum", [P, H])
        sq_mean = sb("sq_mean", [P, H])
        rstd_h = sb("rstd_h", [P, H])
        heads = sb("heads", [P, H, P])
        heads_t = sb("heads_t", [P, H, P])
        heads_high = sb("heads_high", [P, H, P], FP32R)
        heads_low = sb("heads_low", [P, H, P], FP32R)
        x_res = sb("x_res", [P, 2, DM])
        x1 = sb("x1", [P, 2, DM])
        st2 = sb("st2", [P, 6])
        mv2 = sb("mv2", [P, 2])
        rstd2 = sb("rstd2", [P, 1])
        xn2 = sb("xn2", [P, DM])
        xn2_t = sb("xn2_t", [P, KC, P])
        ctx_sb = sb("ctx_sb", [M, 2, DM])
        ctx_t_sb = sb("ctx_t_sb", [P, 2, KC, M])
        mask_bias = sb("mask_bias", [P, M])
        xscore_kept = sb("xscore_kept", [P, M])
        xscore = sb("xscore", [P, M])
        xneg_max = sb("xneg_max", [P, 1])
        xshifted = sb("xshifted", [P, M])
        xprobs = sb("xprobs", [P, M])
        xsum = sb("xsum", [P, 1])
        xprobs_t = sb("xprobs_t", [M, P])
        xinv = sb("xinv", [P, 1])
        xcoef = sb("xcoef", [P, 1])
        x2 = sb("x2", [P, 2, DM])
        st3 = sb("st3", [P, 6])
        mv3 = sb("mv3", [P, 2])
        rstd3 = sb("rstd3", [P, 1])
        row = sb("row", [P, 2, ROW])
        xn3_t = sb("xn3_t", [P, KC, P])
        logits = sb("logits", [P, E])
        top8 = sb("top8", [P, 8])
        rest = sb("rest", [P, E])
        chosen = sb("chosen", [P, E], BF16)
        lneg_max = sb("lneg_max", [P, 1])
        lexp = sb("lexp", [P, E])
        lexp_chosen = sb("lexp_chosen", [P, E])
        wsum = sb("wsum", [P, 1])
        winv = sb("winv", [P, 1])
        taken = sb("taken", [P, E])
        pos = sb("pos", [P, E])
        fits = sb("fits", [P, E])
        second_half = sb("second_half", [P, E])
        address = sb("address", [P, E])
        address2 = sb("address2", [P, E])
        key = sb("key", [P, E])
        slot8 = sb("slot8", [P, 8])
        no_slot = sb("no_slot", [P, 8])
        slot_idx = sb("slot_idx", [P, 2, 8], I32)
        token_id = sb("token_id", [P, 2], I32)

        gu_sb = sb("gu_sb", [P, 2, KC, 2 * INTER])
        dn_sb = sb("dn_sb", [P, 2, DM])
        dn2_sb = sb("dn2_sb", [INTER - P, 2, DM])
        slot_table = sb("slot_table", [HS, E * 2], I32)
        gather_idx = sb("gather_idx", [HS, 2, 2], I32)
        scatter_idx = sb("scatter_idx", [HS, 2, 2], I32)
        rows = w_raw[0:HS, :, :, :].rearrange("p a c n -> p (a c n)")[:, 0:4 * ROW]\
            .rearrange("p (e h n) -> p e h n", e=2, h=2)
        weight_of = [sb("weight_even", [HS, 2]), sb("weight_odd", [HS, 2])]
        rows_t = w_raw[:, :, :, :].rearrange("p a c n -> p (a c n)")[:, 4 * ROW:4 * ROW + 2 * KC * CAP]\
            .rearrange("p (e c n) -> p e c n", e=2, c=KC)
        silu1 = sb("silu1", [P, CAP])
        silu2 = sb("silu2", [INTER - P, CAP])
        h1 = sb("h1", [P, 2, CAP])
        h2 = sb("h2", [INTER - P, 2, CAP])
        y = qk_both[0:HS, :].rearrange("p (e h n) -> p e h n", e=2, h=2)

        ps = stack.enter_context(nc.psum_tensor("ps", [P, 8, DM], FP32))
        bank_ta, bank_tb = ps[:, 0, :], ps[:, 1, :]
        banks_qk = ps[:, 2:4, :]
        bank_r = ps[:, 4, :]
        xscore_ps, logit_ps = bank_r[:, 0:M], bank_r[:, M:M + E]
        count_ps = bank_r[:, 2 * M:2 * M + 2 * E]
        bank_o = ps[:, 5, :]
        banks_s = ps[:, 6:8, :]
        bank_v = ps[:, 6, :]

        def blocks(bank):
            return bank.rearrange("p (c n) -> p c n", n=P)

        s_blank = sem("constants_filled")
        s_made = sem("constants_made")
        d_w = [sem("weights_loaded0"), sem("weights_loaded1")]
        s_rope = sem("rope_table_loaded")
        s_split_a = sem("weights_high_made")
        s_split_v = sem("weights_low_made")
        s_late = sem("late_weights_loaded")
        s_setup_v = sem("setup_by_vector")
        s_setup_pe = sem("setup_by_tensor")
        s_setup_act = sem("setup_by_scalar")
        s_spare = sem("spare_rows_written")
        d_xln = [sem("x_for_norm_loaded0"), sem("x_for_norm_loaded1")]
        d_xres = [sem("x_residual_loaded0"), sem("x_residual_loaded1")]
        d_ctx = [sem("context_loaded0"), sem("context_loaded1")]
        d_row = [sem("records_stored0"), sem("records_stored1")]
        d_x2 = [sem("residual_stored0"), sem("residual_stored1")]
        d_slot = [sem("slots_scattered0"), sem("slots_scattered1")]
        ln1 = Steps(sem("norm1_vector"), "stats aggr eps normed")
        ln1_p = Steps(sem("norm1_pool"), "rstd")
        prj_t = Steps(sem("project_tensor"), "xT q qk v qT kT")
        prj_a = Steps(sem("project_scalar"), "xT v qT kT")
        prj_v = Steps(sem("project_vector"), "low")
        rope = Steps(sem("rope_vector"), "cos sin real imag")
        att_t = Steps(sem("attend_tensor"), "scores diffT pv headsT")
        att_o = Steps(sem("attend_tensor_project"), "proj")
        att_a = Steps(sem("attend_scalar"), "exp diffT square headsT high")
        att_v = Steps(sem("attend_vector"), "max negmax inv coef weighted diff sqsum sqmean heads")
        att_l = Steps(sem("attend_vector_low"), "low")
        att_p = Steps(sem("attend_pool"), "rstd")
        crs_v = Steps(sem("cross_vector"), "x1 stats aggr eps normed bias kept score max shifted")
        crs_p = Steps(sem("cross_pool"), "rstd")
        crs_t = Steps(sem("cross_tensor"), "xT scores probsT readout")
        crs_a = Steps(sem("cross_scalar"), "xT exp probsT")
        out_v = Steps(sem("readout_vector"), "inv coef x2 stats aggr eps normed")
        out_p = Steps(sem("readout_pool"), "rstd")
        rte_t = Steps(sem("route_tensor"), "xT logits counts")
        rte_a = Steps(sem("route_scalar"), "xT exp")
        rte_v = Steps(sem("route_vector"), "logits top8 rest chosen negmax pos taken")
        slt_v = Steps(sem("slots_vector"), "wsum winv fits weights half addr addr2 key slot8 none slots token")
        d_gu = [sem("gate_up_loaded0"), sem("gate_up_loaded1")]
        d_dn = [sem("down_loaded0"), sem("down_loaded1")]
        s_table = sem("slot_table_loaded")
        d_rows = [sem("rows_gathered0"), sem("rows_gathered1")]
        d_add = [sem("outputs_added0"), sem("outputs_added1")]
        ffn_t = Steps(sem("expert_tensor"), "rowsT0 rowsT1")
        gup_t = Steps(sem("gate_up_tensor"), "first second")
        dwn_t = Steps(sem("down_tensor"), "y0 y1")
        ffn_i = Steps(sem("expert_vector_index"), "index")
        ffn_v = Steps(sem("expert_vector_rows"), "weight rowsT1")
        ffn_a = Steps(sem("expert_scalar_rows"), "rowsT0")
        gup_a = Steps(sem("gate_up_scalar"), "silu1 silu2")
        gup_v = Steps(sem("gate_up_vector"), "h1 h2")
        dwn_v = Steps(sem("down_vector"), "index y1")
        dwn_a = Steps(sem("down_scalar"), "y0")

        block = stack.enter_context(nc.Block())

        SKEW = {"norm": 0, "project": 1, "attend": 2, "cross": 3, "route": 4, "slots": 5}
        PAIRS, FIRST, LAST = (NB + 6) // 2, 3, NB // 2

        def turns(eng, turn):
            def trip(pair):
                for j in range(2):
                    turn({k: Batch(pair, j - s, NB) for k, s in SKEW.items()})
            for pair in range(FIRST):
                trip(pair)
            with eng.Fori(FIRST, LAST) as pair:
                trip(pair)
            for pair in range(LAST, PAIRS):
                trip(pair)

        ESKEW = {"gather": 0, "turn": 1, "up": 2, "down": 3}
        EPAIRS, EFIRST, ELAST = (E + 4) // 2, 2, E // 2

        def expert_turns(eng, turn):
            def trip(pair):
                for j in range(2):
                    turn({k: Batch(pair, j - s, E) for k, s in ESKEW.items()})
            for pair in range(EFIRST):
                trip(pair)
            with eng.Fori(EFIRST, ELAST) as pair:
                trip(pair)
            for pair in range(ELAST, EPAIRS):
                trip(pair)

        s_paced = {nc.vector.engine: sem("vector_paced"), nc.gpsimd.engine: sem("pool_paced"),
                   nc.scalar.engine: sem("scalar_paced")}

        def settled(eng):
            eng.sem_inc(s_paced[eng.engine], 1)

        @block.sync
        def _(sp):
            for m in range(4):
                if m >= 2:
                    sp.wait_ge(s_split_v, m - 1)
                sp.dma_start(w_raw[:, m % 2, :, :], weights[m * P:(m + 1) * P, :, :]).then_inc(d_w[m % 2], 16)
            sp.dma_start(rope_tab[:, :, :], cos_sin).then_inc(s_rope, 16)

            def turn(b):
                n, c, r, s = b["norm"], b["cross"], b["route"], b["slots"]
                if n.exists():
                    wait(sp, ln1, n.back(2), "normed")
                    sp.dma_start(x_ln[:, n.parity, :], x[bass.ds(n.index * P, P), :])\
                      .then_inc(d_xln[n.parity], 16)
                if c.exists():
                    wait(sp, crs_v, c.back(2), "x1")
                    sp.dma_start(x_res[:, c.parity, :], x[bass.ds(c.index * P, P), :])\
                      .then_inc(d_xres[c.parity], 16)
                    wait(sp, crs_t, c.back(2), "readout")
                    sp.dma_start(ctx_t_sb[:, c.parity, :, :], ctx_t[bass.ds(c.index * P, P), :, :])\
                      .then_inc(d_ctx[c.parity], 16)
                    sp.dma_start(ctx_sb[:, c.parity, :], ctx_rows[bass.ds(c.index * M, M), :])\
                      .then_inc(d_ctx[c.parity], 16)
                if r.exists():
                    wait(sp, out_v, r, "x2")
                    sp.dma_start(out[bass.ds(r.index * P, P), :], x2[:, r.parity, :])\
                      .then_inc(d_x2[r.parity], 16)
                if s.exists():
                    wait(sp, slt_v, s, "weights")
                    sp.dma_start(xw[bass.ds(s.index * P, P), :], row[:, s.parity, :])\
                      .then_inc(d_row[s.parity], 16)
            turns(sp, turn)

            for par in range(2):
                sp.wait_ge(d_slot[par], 16 * 8 * NB // 2)
                sp.wait_ge(d_row[par], 16 * NB // 2)
                sp.wait_ge(d_x2[par], 16 * NB // 2)
            sp.dma_start(slot_table[:, :], table.rearrange("(p n) o -> p (n o)", p=HS)).then_inc(s_table, 16)

            def expert_turn(b):
                e, t = b["gather"], b["turn"]
                if e.exists():
                    wait(sp, gup_t, e.back(2), "second")
                    sp.dma_start(gu_sb[:, e.parity, :, :], gate_up[bass.ds(e.index * P, P), :, :])\
                      .then_inc(d_gu[e.parity], 16)
                if t.exists():
                    wait(sp, dwn_t, t.back(2), "y1")
                    sp.dma_start(dn_sb[:, t.parity, :], down_proj[bass.ds(t.index * INTER, P), :])\
                      .then_inc(d_dn[t.parity], 16)
                    sp.dma_start(dn2_sb[:, t.parity, :],
                                 down_proj[bass.ds(t.index * INTER + P, INTER - P), :])\
                      .then_inc(d_dn[t.parity], 16)
            expert_turns(sp, expert_turn)
            for par in range(2):
                sp.wait_ge(d_add[par], 16 * 2 * E // 2)

        @block.gpsimd
        def _(pool):
            pool.memset(ident[:, :], 0.0).then_inc(s_blank, 1)
            pool.memset(ones[:, :], 1.0)
            pool.memset(before_bf[:, :], 1.0).then_inc(s_blank, 1)
            pool.memset(neg_half[:, :], -0.5)
            pool.memset(zeros, 0.0)
            pool.iota(token_ids[:, :], [[P, NB]], base=0, channel_multiplier=1)
            pool.iota(spare_ids[:, :, :], [[0, E], [HS, 2]], base=T, channel_multiplier=1)
            pool.iota(expert_iota[:, :], [[1, E]], base=0, channel_multiplier=0,
                      allow_small_or_imprecise_dtypes=True)
            pool.iota(slot_base[:, :], [[2, E]], base=1, channel_multiplier=0,
                      allow_small_or_imprecise_dtypes=True)
            pool.memset(ones_bf[:, :], 1.0)
            pool.wait_ge(s_blank, 2)
            pool.affine_select(out=ident[:, :], in_=ident[:, :], compare_op=ALU.not_equal, fill=1.0, base=0,
                               pattern=[[-1, P]], channel_multiplier=1)
            pool.affine_select(out=before_bf[:, :], in_=before_bf[:, :], compare_op=ALU.is_gt, fill=0.0,
                               base=0, pattern=[[1, P]], channel_multiplier=-1).then_inc(s_made, 1)
            pool.wait_ge(s_made, 1)
            pool.dma_start(table.rearrange("(p n) o -> p (n o)", p=HS),
                           spare_ids[:, :, :].rearrange("p e h -> p (e h)")).then_inc(s_spare, 16)
            pool.dma_start(xw[T:T + CAP, :].rearrange("(p a) n -> p (a n)", a=2), zeros)\
                .then_inc(s_spare, 16)
            pool.dma_start(out[T:T + CAP, :].rearrange("(p a) n -> p (a n)", a=2), zeros[:, 0:2 * DM])\
                .then_inc(s_spare, 16)
            pool.wait_ge(s_spare, 48)

            def turn(b):
                n, a, c, o, s = b["norm"], b["attend"], b["cross"], b["route"], b["slots"]

                def scatter(k0):
                    for k in range(k0, k0 + 2):
                        pool.indirect_dma_start(
                            out=table, out_offset=bass.IndirectOffsetOnAxis(ap=slot_idx[:, s.parity, k:k + 1], axis=0),
                            in_=token_id[:, s.parity:s.parity + 1], in_offset=None,
                            bounds_check=SLOTS - 1, oob_is_err=False).then_inc(d_slot[s.parity], 16)

                if o.exists():
                    wait(pool, out_v, o, "eps")
                    pool.tensor_tensor(rstd3[:, :], mv3[:, 1:2], neg_half[:, 0:1], ALU.pow)\
                        .then_inc(out_p.sem, 1)
                if n.exists():
                    wait(pool, ln1, n, "eps")
                    pool.tensor_tensor(rstd1[:, :], mv1[:, 1:2], neg_half[:, 0:1], ALU.pow)\
                        .then_inc(ln1_p.sem, 1)
                if s.exists():
                    wait(pool, slt_v, s, "token")
                    settled(pool)
                    scatter(0)
                if c.exists():
                    wait(pool, crs_v, c, "eps")
                    pool.tensor_tensor(rstd2[:, :], mv2[:, 1:2], neg_half[:, 0:1], ALU.pow)\
                        .then_inc(crs_p.sem, 1)
                if s.exists():
                    scatter(2)
                    scatter(4)
                    scatter(6)
                if a.exists():
                    wait(pool, att_v, a, "sqmean")
                    pool.tensor_tensor(rstd_h[:, :], sq_mean[:, :], neg_half[:, :], ALU.pow)\
                        .then_inc(att_p.sem, 1)
            turns(pool, turn)

            def gather(e):
                wait(pool, ffn_i, e, "index")
                wait(pool, ffn_t, e.back(2), "rowsT1")
                wait(pool, ffn_v, e.back(2), "weight")
                settled(pool)
                for h in range(2):
                    pool.indirect_dma_start(
                        out=rows[:, e.parity, h, :], out_offset=None, in_=xw,
                        in_offset=bass.IndirectOffsetOnAxis(ap=gather_idx[:, e.parity, h:h + 1], axis=0),
                        bounds_check=T + CAP - 1, oob_is_err=True).then_inc(d_rows[e.parity], 16)

            def expert_turn(b):
                g, d = b["gather"], b["down"]
                if g.exists():
                    gather(g)
                if d.exists():
                    wait_dma(pool, d_add, d.back(1), 2)
                    wait(pool, dwn_a, d, "y0")
                    wait(pool, dwn_v, d, "y1")
                    settled(pool)
                    for h in range(2):
                        pool.indirect_dma_start(
                            out=out, out_offset=bass.IndirectOffsetOnAxis(ap=scatter_idx[:, d.parity, h:h + 1], axis=0),
                            in_=y[:, d.parity, h, :], in_offset=None,
                            bounds_check=T + CAP - 1, oob_is_err=True,
                            compute_op=ALU.add).then_inc(d_add[d.parity], 16)
            expert_turns(pool, expert_turn)

        @block.scalar
        def _(act):
            for n in range(4):
                act.dma_start(lam_in[:, n, :], lambdas[n].partition_broadcast(P)).then_inc(s_late, 16)
            act.dma_start(subln_sb[:, :], subln.rearrange("(p o) -> p o", o=1)).then_inc(s_late, 16)
            act.dma_start(o2n_i[:, :], old_to_new.rearrange("(p o) -> p o", o=1)).then_inc(s_late, 16)
            act.dma_start(gate_sb[:, :], gate).then_inc(s_late, 16)
            act.dma_start(mask_sb[:, :], mask.partition_broadcast(P)).then_inc(s_late, 16)
            act.wait_ge(s_setup_v, 2)
            act.activation(lam_exp[:, :], lam_sum[:, :], ACT.Exp).then_inc(s_setup_act, 1)

            def copy(dst, src, steps, scale=None):
                if scale is None:
                    act.activation(dst, src, ACT.Copy).then_inc(steps.sem, 1)
                else:
                    act.activation(dst, src, ACT.Copy, scale=scale).then_inc(steps.sem, 1)

            for m in range(4):
                act.wait_ge(d_w[m % 2], 16 * (m // 2 + 1))
                act.activation(w_high[:, m, :, :], w_raw[:, m % 2, :, :], ACT.Copy).then_inc(s_split_a, 1)

            def turn(b):
                p, a, c, r = b["project"], b["attend"], b["cross"], b["route"]
                if p.exists():
                    wait(act, prj_t, p, "xT")
                    wait(act, prj_t, p.back(1), "v")
                    wait(act, prj_v, p.back(1), "low")
                    copy(xn1_high[:, :, :], blocks(bank_ta), prj_a)
                if a.exists():
                    wait(act, att_v, a, "negmax")
                    wait(act, att_v, a.back(1), "weighted")
                    for s in range(2):
                        for h in range(H):
                            last = act.activation(probs[:, s, h, :], blocks(banks_s[:, s, :])[:, h, :], ACT.Exp,
                                                  bias=neg_max_s[:, s, h:h + 1], scale=INV_SCALING,
                                                  accum_out=prob_sum[:, s, h:h + 1])
                    last.then_inc(att_a.sem, 1)
                if r.exists():
                    wait(act, rte_t, r, "xT")
                    copy(xn3_t[:, :, :], blocks(bank_tb), rte_a)
                if c.exists():
                    wait(act, crs_t, c, "xT")
                    copy(xn2_t[:, :, :], blocks(bank_ta), crs_a)
                if a.exists():
                    wait(act, att_t, a, "diffT")
                    copy(diff_t[:, :, :], blocks(bank_tb), att_a)
                if r.exists():
                    wait(act, rte_v, r, "negmax")
                    wait(act, slt_v, r.back(1), "wsum")
                    act.activation(lexp[:, :], logits[:, :], ACT.Exp, bias=lneg_max[:, :])\
                        .then_inc(rte_a.sem, 1)
                if a.exists():
                    wait(act, att_t, a, "pv")
                    act.activation(squares[:, :, :], blocks(bank_o), ACT.Square).then_inc(att_a.sem, 1)
                if c.exists():
                    wait(act, crs_v, c, "shifted")
                    wait(act, out_v, c.back(1), "inv")
                    act.activation(xprobs[:, :], xshifted[:, :], ACT.Exp, scale=XSCALE,
                                   accum_out=xsum[:, :]).then_inc(crs_a.sem, 1)
                if p.exists():
                    wait(act, prj_t, p, "v")
                    wait(act, att_t, p.back(2), "pv")
                    copy(v_sb[:, p.parity, :], bank_v, prj_a)
                if c.exists():
                    wait(act, crs_t, c, "probsT")
                    copy(xprobs_t[:, :], bank_ta[:, 0:P], crs_a)
                if p.exists():
                    wait(act, prj_t, p, "qT")
                    wait(act, att_t, p.back(1), "scores")
                    copy(q_t[:, :, :], blocks(bank_tb), prj_a)
                    wait(act, prj_t, p, "kT")
                    copy(k_t[:, :, :], blocks(bank_ta), prj_a)
                if a.exists():
                    wait(act, att_t, a, "headsT")
                    wait(act, att_l, a.back(1), "low")
                    copy(heads_t[:, :, :], blocks(bank_tb), att_a, scale=subln_sb[:, :])
                    wait(act, att_a, a, "headsT")
                    wait(act, att_o, a.back(1), "proj")
                    copy(heads_high[:, :, :], heads_t[:, :, :], att_a)
            act.wait_ge(s_late, 16 * 8)
            turns(act, turn)

            def expert_turn(b):
                g, u, d = b["turn"], b["up"], b["down"]
                if u.exists():
                    wait(act, gup_t, u, "first")
                    wait(act, gup_v, u.back(1), "h2")
                    act.activation(silu1[:, :], ps[:, 2, 0:CAP], ACT.Silu).then_inc(gup_a.sem, 1)
                    wait(act, gup_t, u, "second")
                    act.activation(silu2[:, :], ps[0:INTER - P, 3, 0:CAP], ACT.Silu).then_inc(gup_a.sem, 1)
                if d.exists():
                    wait(act, dwn_t, d, "y0")
                    wait(act, ffn_v, d, "weight")
                    wait_dma(act, d_add, d.back(2), 2)
                    copy(y[:, d.parity, 0, :], ps[0:HS, 4, :], dwn_a, scale=weight_of[d.parity][:, 0:1])
                if g.exists():
                    wait(act, ffn_t, g, "rowsT0")
                    wait(act, gup_t, g.back(2), "second")
                    copy(rows_t[:, g.parity, :, 0:HS], ps[:, 0, 0:KC * HS].rearrange("p (c n) -> p c n", c=KC),
                         ffn_a)
            expert_turns(act, expert_turn)

        @block.vector
        def _(dve):
            dve.wait_ge(s_late, 16 * 8)
            dve.tensor_tensor(lam_prod[:, :, :], lam_in[:, 0:2, :], lam_in[:, 2:4, :], ALU.mult)\
                .then_inc(s_setup_v, 1)
            dve.wait_ge(s_setup_v, 1)
            dve.reduce_sum(lam_sum[:, :], lam_prod[:, :, :], AX.X).then_inc(s_setup_v, 1)
            dve.tensor_copy(o2n_f[:, :], o2n_i[:, :]).then_inc(s_setup_v, 1)
            dve.reduce_max(valid[:, :], mask_sb[:, :].rearrange("p (b m) -> p b m", m=M), AX.X)\
                .then_inc(s_setup_v, 1)
            dve.memset(taken[:, :], 0.0)
            dve.wait_ge(s_setup_v, 4)
            dve.wait_ge(s_made, 1)
            dve.tensor_scalar(is_new[:, :], expert_iota[:, :], o2n_f[:, :], None, ALU.is_equal)\
                .then_inc(s_setup_v, 1)
            dve.wait_ge(s_setup_act, 1)
            dve.tensor_tensor(lam_gap[:, :], lam_exp[:, 1:2], lam_exp[:, 0:1], ALU.subtract)\
                .then_inc(s_setup_v, 1)
            dve.wait_ge(s_setup_v, 6)
            dve.tensor_scalar_add(neg_lam[:, :], lam_gap[:, :], -LAMBDA_INIT).then_inc(s_setup_v, 1)
            dve.wait_ge(s_setup_pe, 1)
            dve.tensor_copy(gate_new[:, :, :], ps[:, 0, 0:KC * E].rearrange("p (c e) -> p c e", c=KC))\
                .then_inc(s_setup_v, 1)
            dve.tensor_scalar(absent_bias[:, :], ps[:, 1, 0:E], -1.0, BIG, ALU.add, ALU.mult)\
                .then_inc(s_setup_v, 1)
            dve.wait_ge(s_setup_v, 9)

            def step(steps, ins):
                ins.then_inc(steps.sem, 1)

            def norm_stats(steps, b, src, st, mv):
                step(steps, dve.bn_stats(st[:, :], src))
                wait(dve, steps, b, "stats")
                settled(dve)
                step(steps, dve.bn_aggr(mv[:, :], st[:, :]))
                wait(dve, steps, b, "aggr")
                step(steps, dve.tensor_scalar_add(mv[:, 1:2], mv[:, 1:2], EPS))

            for m in range(4):
                dve.wait_ge(s_split_a, m + 1)
                dve.tensor_tensor(w_low[:, m, :, :], w_raw[:, m % 2, :, :], w_high[:, m, :, :].bitcast(FP32),
                                  ALU.subtract).then_inc(s_split_v, 1)
            dve.wait_ge(s_rope, 16)
            dve.wait_ge(s_spare, 48)

            def turn(b):
                n, p, a, c, r, s = (b[k] for k in ("norm", "project", "attend", "cross", "route", "slots"))
                if r.exists():
                    wait(dve, crs_a, r, "exp")
                    step(out_v, dve.reciprocal(xinv[:, :], xsum[:, :]))
                if s.exists():
                    wait(dve, rte_a, s, "exp")
                    step(slt_v, dve.scalar_tensor_tensor(lexp_chosen[:, :], lexp[:, :], 1.0, chosen[:, :],
                                                         ALU.mult, ALU.mult, accum_out=wsum[:, :]))
                if r.exists():
                    wait(dve, out_v, r, "inv")
                    step(out_v, dve.tensor_scalar(xcoef[:, :], valid[:, bass.ds(r.index, 1)], xinv[:, :], None,
                                                  ALU.mult))
                if s.exists():
                    wait(dve, slt_v, s, "wsum")
                    step(slt_v, dve.reciprocal(winv[:, :], wsum[:, :]))
                    step(slt_v, dve.scalar_tensor_tensor(fits[:, :], pos[:, :], float(CAP), chosen[:, :],
                                                         ALU.is_lt, ALU.mult))
                if r.exists():
                    wait(dve, out_v, r, "coef")
                    wait(dve, crs_t, r, "readout")
                    wait_dma(dve, d_x2, r.back(2), 1)
                    step(out_v, dve.scalar_tensor_tensor(x2[:, r.parity, :], bank_r, xcoef[:, :], x1[:, r.parity, :],
                                                         ALU.mult, ALU.add))
                if s.exists():
                    wait(dve, slt_v, s, "winv")
                    step(slt_v, dve.tensor_scalar(row[:, s.parity, DM:ROW], lexp_chosen[:, :], winv[:, :], None,
                                                  ALU.mult))
                    step(slt_v, dve.tensor_scalar(second_half[:, :], pos[:, :], float(HS), float(1 - 2 * E * HS),
                                                  ALU.is_ge, ALU.mult))
                    step(slt_v, dve.scalar_tensor_tensor(address[:, :], pos[:, :], float(2 * E), slot_base[:, :],
                                                         ALU.mult, ALU.add))
                if c.exists():
                    wait(dve, att_a, c, "high")
                    wait(dve, att_o, c.back(1), "proj")
                    step(att_l, dve.tensor_tensor(heads_low[:, :, :], heads_t[:, :, :],
                                                  heads_high[:, :, :].bitcast(FP32), ALU.subtract))
                if p.exists():
                    wait(dve, prj_a, p, "xT")
                    wait(dve, prj_t, p.back(1), "v")
                    step(prj_v, dve.tensor_tensor(xn1_low[:, :, :], blocks(bank_ta), xn1_high[:, :, :].bitcast(FP32),
                                                  ALU.subtract))
                if s.exists():
                    wait(dve, slt_v, s, "addr")
                    step(slt_v, dve.tensor_tensor(address2[:, :], address[:, :], second_half[:, :], ALU.add))
                if r.exists():
                    wait(dve, out_v, r, "x2")
                    step(out_v, dve.bn_stats(st3[:, :], x2[:, r.parity, :]))
                if s.exists():
                    wait(dve, slt_v, s, "addr2")
                    step(slt_v, dve.tensor_tensor(key[:, :], address2[:, :], fits[:, :], ALU.mult))
                if a.exists():
                    wait(dve, att_t, a, "scores")
                    wait(dve, att_a, a.back(1), "exp")
                    step(att_v, dve.tensor_reduce(neg_max[:, :, :], banks_s.rearrange("p s (h n) -> p s h n", n=P),
                                                  AX.X, ALU.max, negate=True))
                if r.exists():
                    wait(dve, out_v, r, "stats")
                    settled(dve)
                    step(out_v, dve.bn_aggr(mv3[:, :], st3[:, :]))
                if a.exists():
                    wait(dve, att_v, a, "max")
                    step(att_v, dve.tensor_scalar_mul(neg_max_s[:, :, :], neg_max[:, :, :], INV_SCALING))
                if r.exists():
                    wait(dve, out_v, r, "aggr")
                    step(out_v, dve.tensor_scalar_add(mv3[:, 1:2], mv3[:, 1:2], EPS))
                if s.exists():
                    wait(dve, slt_v, s, "key")
                    settled(dve)
                    step(slt_v, dve.max(slot8[:, :], key[:, :]))
                if n.exists():
                    wait_dma(dve, d_xln, n, 1)
                    step(ln1, dve.bn_stats(st1[:, :], x_ln[:, n.parity, :]))
                if s.exists():
                    wait(dve, slt_v, s, "slot8")
                    step(slt_v, dve.tensor_scalar(no_slot[:, :], slot8[:, :], 0.0, 1e6, ALU.is_equal, ALU.mult))
                if n.exists():
                    wait(dve, ln1, n, "stats")
                    settled(dve)
                    step(ln1, dve.bn_aggr(mv1[:, :], st1[:, :]))
                if s.exists():
                    wait(dve, slt_v, s, "none")
                    wait_dma(dve, d_slot, s.back(2), 8)
                    step(slt_v, dve.scalar_tensor_tensor(slot_idx[:, s.parity, :], no_slot[:, :], -1.0, slot8[:, :],
                                                         ALU.add, ALU.add))
                    step(slt_v, dve.tensor_scalar_add(token_id[:, s.parity:s.parity + 1],
                                                      token_ids[:, bass.ds(s.index, 1)], 0.0))
                if n.exists():
                    wait(dve, ln1, n, "aggr")
                    step(ln1, dve.tensor_scalar_add(mv1[:, 1:2], mv1[:, 1:2], EPS))
                if c.exists():
                    wait_dma(dve, d_xres, c, 1)
                    wait(dve, att_o, c, "proj")
                    step(crs_v, dve.tensor_tensor(x1[:, c.parity, :], bank_o, x_res[:, c.parity, :], ALU.add))
                if r.exists():
                    wait(dve, out_p, r, "rstd")
                    wait_dma(dve, d_row, r.back(2), 1)
                    step(out_v, dve.tensor_scalar(row[:, r.parity, 0:DM], x2[:, r.parity, :], mv3[:, 0:1], rstd3[:, :],
                                                  ALU.subtract, ALU.mult))
                if c.exists():
                    wait(dve, crs_v, c, "x1")
                    norm_stats(crs_v, c, x1[:, c.parity, :], st2, mv2)
                if n.exists():
                    wait(dve, ln1_p, n, "rstd")
                    wait(dve, prj_t, n.back(2), "xT")
                    step(ln1, dve.tensor_scalar(xn1[:, n.parity, :], x_ln[:, n.parity, :], mv1[:, 0:1], rstd1[:, :],
                                                ALU.subtract, ALU.mult))
                if a.exists():
                    wait(dve, att_a, a, "exp")
                    step(att_v, dve.reciprocal(coef[:, :, :], prob_sum[:, :, :]))
                    wait(dve, att_v, a, "inv")
                    step(att_v, dve.tensor_scalar(coef[:, 1, :], coef[:, 1, :], neg_lam[:, :], None, ALU.mult))
                    wait(dve, att_v, a, "coef")
                    step(att_v, dve.tensor_tensor(
                        weighted[:, :, :, :].rearrange("p s h n -> p (s h) n"),
                        probs[:, :, :, :].rearrange("p s h n -> p (s h) n"),
                        coef[:, :, :].rearrange("p s h -> p (s h)").unsqueeze(2).to_broadcast([P, 2 * H, P]),
                        ALU.mult))
                    wait(dve, att_v, a, "weighted")
                    wait(dve, att_t, a.back(1), "diffT")
                    step(att_v, dve.tensor_tensor(diff[:, :, :], weighted[:, 0, :, :], weighted[:, 1, :, :], ALU.add))
                if c.exists():
                    wait(dve, crs_p, c, "rstd")
                    wait(dve, crs_t, c.back(1), "xT")
                    step(crs_v, dve.tensor_scalar(xn2[:, :], x1[:, c.parity, :], mv2[:, 0:1], rstd2[:, :],
                                                  ALU.subtract, ALU.mult))
                    mask_row = mask_sb[:, bass.ds(c.index * M, M)]
                    wait(dve, crs_v, c.back(1), "score")
                    step(crs_v, dve.tensor_scalar(mask_bias[:, :], mask_row, -1.0, BIG, ALU.add, ALU.mult))
                if p.exists():
                    qk = banks_qk.rearrange("p a (g f) -> p (a g) f", f=NF)
                    wait(dve, prj_t, p, "qk")
                    for name, buf, i in (("cos", qk_cos, 0), ("sin", qk_sin, 1)):
                        step(rope, dve.tensor_tensor(
                            buf[:, :, :, :].rearrange("p g r f -> p (g r) f"), qk,
                            rope_tab[:, i:i + 1, :].to_broadcast([P, 4 * NH2, NF]), ALU.mult))
                if r.exists():
                    wait(dve, rte_t, r, "logits")
                    wait(dve, crs_t, c, "scores")
                    wait(dve, rte_a, r.back(1), "exp")
                    step(rte_v, dve.tensor_tensor(logits[:, :], logit_ps, absent_bias[:, :], ALU.add))
                    wait(dve, rte_v, r, "logits")
                    settled(dve)
                    step(rte_v, dve.max(top8[:, :], logits[:, :]))
                    wait(dve, rte_v, r, "top8")
                    settled(dve)
                    step(rte_v, dve.match_replace(rest[:, :], top8[:, :], logits[:, :], -3e38))
                    wait(dve, rte_v, r, "rest")
                    step(rte_v, dve.tensor_tensor(chosen[:, :], rest[:, :], logits[:, :], ALU.is_lt))
                    step(rte_v, dve.tensor_scalar_mul(lneg_max[:, :], top8[:, 0:1], -1.0))
                if p.exists():
                    wait(dve, rope, p, "sin")
                    wait(dve, prj_t, p.back(1), "kT")
                    step(rope, dve.tensor_tensor(qk_rot[:, :, 0, :], qk_cos[:, :, 0, :], qk_sin[:, :, 1, :],
                                                 ALU.subtract))
                    step(rope, dve.tensor_tensor(qk_rot[:, :, 1, :], qk_cos[:, :, 1, :], qk_sin[:, :, 0, :], ALU.add))
                if c.exists():
                    wait(dve, crs_t, c, "scores")
                    step(crs_v, dve.tensor_tensor(xscore_kept[:, :], xscore_ps, mask_row, ALU.mult))
                    wait(dve, crs_v, c, "kept")
                    step(crs_v, dve.tensor_tensor(xscore[:, :], xscore_kept[:, :], mask_bias[:, :], ALU.add))
                    wait(dve, crs_v, c, "score")
                    step(crs_v, dve.tensor_reduce(xneg_max[:, :], xscore[:, :], AX.X, ALU.max, negate=True))
                    wait(dve, crs_v, c, "max")
                    wait(dve, crs_a, c.back(1), "exp")
                    step(crs_v, dve.tensor_scalar(xshifted[:, :], xscore[:, :], xneg_max[:, :], None, ALU.add))
                if a.exists():
                    wait(dve, att_a, a, "square")
                    step(att_v, dve.reduce_sum(sq_sum[:, :], squares[:, :, :], AX.X))
                    wait(dve, att_v, a, "sqsum")
                    step(att_v, dve.tensor_scalar(sq_mean[:, :], sq_sum[:, :], 1.0 / P, EPS, ALU.mult, ALU.add))
                if r.exists():
                    wait(dve, rte_t, r, "counts")
                    step(rte_v, dve.tensor_tensor(pos[:, :], count_ps[:, 0:E], taken[:, :], ALU.add))
                    wait(dve, rte_v, r, "pos")
                    step(rte_v, dve.tensor_tensor(taken[:, :], count_ps[:, E:2 * E], taken[:, :], ALU.add))
                if a.exists():
                    wait(dve, att_p, a, "rstd")
                    wait(dve, att_t, a.back(1), "headsT")
                    step(att_v, dve.tensor_tensor(heads[:, :, :], blocks(bank_o),
                                                  rstd_h[:, :].unsqueeze(2).to_broadcast([P, H, P]), ALU.mult))
            turns(dve, turn)

            dve.wait_ge(s_table, 16)

            def expert_turn(b):
                g, t, u, d = b["gather"], b["turn"], b["up"], b["down"]
                if g.exists():
                    wait_dma(dve, d_rows, g.back(2), 2)
                    step(ffn_i, dve.tensor_scalar_add(gather_idx[:, g.parity, :], slot_table[:, bass.ds(2 * g.index, 2)],
                                                      0.0))
                if d.exists():
                    wait_dma(dve, d_add, d.back(2), 2)
                    step(dwn_v, dve.tensor_scalar_add(scatter_idx[:, d.parity, :], slot_table[:, bass.ds(2 * d.index, 2)],
                                                      0.0))
                if u.exists():
                    wait(dve, gup_a, u, "silu1")
                    wait(dve, dwn_t, u.back(2), "y1")
                    step(gup_v, dve.tensor_tensor(h1[:, u.parity, :], silu1[:, :], ps[:, 2, CAP:2 * CAP], ALU.mult))
                    wait(dve, gup_a, u, "silu2")
                    step(gup_v, dve.tensor_tensor(h2[:, u.parity, :], silu2[:, :], ps[INTER - P:P, 3, 0:CAP], ALU.mult))
                if d.exists():
                    wait(dve, dwn_t, d, "y1")
                    step(dwn_v, dve.tensor_scalar(y[:, d.parity, 1, :], ps[0:HS, 5, :], weight_of[d.parity][:, 1:2], None,
                                                  ALU.mult))
                if t.exists():
                    wait_dma(dve, d_rows, t, 2)
                    wait(dve, dwn_a, t.back(2), "y0")
                    wait(dve, dwn_v, t.back(2), "y1")
                    settled(dve)
                    step(ffn_v, dve.tensor_copy(weight_of[t.parity][:, :], rows[:, t.parity, :, bass.ds(t.index + DM, 1)]
                                                .rearrange("p h o -> p (h o)")))
                    wait(dve, ffn_t, t, "rowsT1")
                    wait(dve, gup_t, t.back(2), "second")
                    step(ffn_v, dve.tensor_copy(rows_t[:, t.parity, :, HS:CAP],
                                                ps[:, 1, 0:KC * HS].rearrange("p (c n) -> p c n", c=KC)))
            expert_turns(dve, expert_turn)

        @block.tensor
        def _(pe):
            pe.wait_ge(s_setup_v, 5)
            for c in range(KC):
                pe.matmul(ps[:, 0, c * E:(c + 1) * E], gate_sb[:, c * P:(c + 1) * P], is_new[:, :],
                          start=True, stop=True)
            pe.matmul(ps[:, 1, 0:E], ones[:, :], is_new[:, :], start=True, stop=True).then_inc(s_setup_pe, 1)
            pe.wait_ge(s_setup_v, 9)
            pe.wait_ge(s_split_v, 4)

            def step(steps, ins):
                ins.then_inc(steps.sem, 1)

            def transpose4(bank, src):
                for c in range(KC):
                    last = pe.transpose(blocks(bank)[:, c, :], src(c), ident[:, :])
                return last

            def product(dst, left, right, n=KC):
                for c in range(n):
                    last = pe.matmul(dst, left(c), right(c), start=(c == 0), stop=(c == n - 1))
                return last

            def product_r(dst, high, low, m):
                parts = [(high, w_high), (high, w_low), (low, w_high)]
                for n, (left, right) in enumerate(parts):
                    for c in range(KC):
                        last = pe.matmul(dst, left[:, c, :], right[:, m, c, :], start=(n == 0 and c == 0),
                                         stop=(n == 2 and c == KC - 1))
                        if n == 1 and c == KC - 1:
                            yield None
                yield last

            def turn(b):
                p, a, c, r = b["project"], b["attend"], b["cross"], b["route"]
                if p.exists():
                    wait(pe, ln1, p, "normed")
                    wait(pe, prj_a, p.back(1), "kT")
                    step(prj_t, transpose4(bank_ta, lambda k: xn1[:, p.parity, k * P:(k + 1) * P]))
                if a.exists():
                    wait(pe, prj_a, a, "kT")
                    wait(pe, prj_a, a, "v")
                    wait(pe, att_a, a.back(1), "exp")
                    for h in range(H):
                        for s in range(2):
                            half = slice(s * HALF, (s + 1) * HALF)
                            last = pe.matmul(blocks(banks_s[:, s, :])[:, h, :], q_t[half, h, :], k_t[half, h, :],
                                             start=True, stop=True)
                    step(att_t, last)
                if c.exists():
                    wait(pe, att_a, c, "high")
                    proj = product_r(bank_o, heads_high, heads_low, W_OUT)
                    next(proj)
                    wait(pe, att_l, c, "low")
                    step(att_o, next(proj))
                if p.exists():
                    wait(pe, rope, p.back(1), "sin")
                    q = product_r(banks_qk[:, 0, :], xn1_high, xn1_low, W_Q)
                    wait(pe, prj_a, p, "xT")
                    next(q)
                    wait(pe, prj_v, p, "low")
                    step(prj_t, next(q))
                if r.exists():
                    wait(pe, out_v, r, "normed")
                    wait(pe, att_a, a.back(1), "headsT")
                    step(rte_t, transpose4(bank_tb, lambda k: row[:, r.parity, k * P:(k + 1) * P]))
                if p.exists():
                    k = product_r(banks_qk[:, 1, :], xn1_high, xn1_low, W_K)
                    next(k)
                    step(prj_t, next(k))
                if c.exists():
                    wait(pe, crs_v, c, "normed")
                    wait(pe, prj_v, p, "low")
                    step(crs_t, transpose4(bank_ta, lambda k: xn2[:, k * P:(k + 1) * P]))
                if r.exists():
                    wait(pe, rte_a, r, "xT")
                    wait(pe, out_v, r, "x2")
                    step(rte_t, product(logit_ps, lambda k: xn3_t[:, k, :], lambda k: gate_new[:, k, :]))
                if c.exists():
                    wait(pe, crs_a, c, "xT")
                    wait_dma(pe, d_ctx, c, 2)
                    step(crs_t, product(xscore_ps, lambda k: xn2_t[:, k, :], lambda k: ctx_t_sb[:, c.parity, k, :]))
                if a.exists():
                    wait(pe, att_v, a, "diff")
                    wait(pe, rte_a, r, "xT")
                    step(att_t, transpose4(bank_tb, lambda k: diff[:, k, :]))
                if p.exists():
                    wait(pe, att_a, a, "exp")
                    v = product_r(bank_v, xn1_high, xn1_low, W_V)
                    next(v)
                if a.exists():
                    wait(pe, att_a, a, "diffT")
                    wait(pe, crs_v, c, "x1")
                    for h in range(H):
                        last = pe.matmul(blocks(bank_o)[:, h, :], diff_t[:, h, :],
                                         v_sb[:, a.parity, h * P:(h + 1) * P], start=True, stop=True)
                    step(att_t, last)
                if p.exists():
                    step(prj_t, next(v))
                if r.exists():
                    wait(pe, rte_v, r, "chosen")
                    wait(pe, crs_v, c, "kept")
                    pe.matmul(count_ps[:, 0:E], before_bf[:, :], chosen[:, :], start=True, stop=True)
                    step(rte_t, pe.matmul(count_ps[:, E:2 * E], ones_bf[:, :], chosen[:, :], start=True, stop=True))
                if c.exists():
                    wait(pe, crs_a, c, "exp")
                    step(crs_t, pe.transpose(bank_ta[:, 0:P], xprobs[:, :], ident[:, :]))
                if p.exists():
                    wait(pe, rope, p, "imag")
                    wait(pe, att_a, a, "diffT")
                    rot = qk_rot[:, :, :, :].rearrange("p g r f -> p (g r f)")
                    step(prj_t, transpose4(bank_tb, lambda k: rot[:, k * P:(k + 1) * P]))
                    wait(pe, crs_a, c, "probsT")
                    step(prj_t, transpose4(bank_ta, lambda k: rot[:, DM + k * P:DM + (k + 1) * P]))
                if c.exists():
                    wait(pe, crs_a, c, "probsT")
                    wait(pe, rte_v, r, "taken")
                    step(crs_t, pe.matmul(bank_r, xprobs_t[:, :], ctx_sb[:, c.parity, :], start=True, stop=True))
                if a.exists():
                    wait(pe, att_v, a, "heads")
                    wait(pe, prj_a, p, "qT")
                    step(att_t, transpose4(bank_tb, lambda k: heads[:, k, :]))
            turns(pe, turn)

            def expert_turn(b):
                g, u, d = b["turn"], b["up"], b["down"]
                if u.exists():
                    wait_dma(pe, d_gu, u, 1)
                    wait(pe, ffn_a, u, "rowsT0")
                    wait(pe, ffn_v, u, "rowsT1")
                    wait(pe, gup_v, u.back(1), "h2")
                    for m in range(2):
                        last = product(ps[:, 2, m * CAP:(m + 1) * CAP],
                                       lambda k: gu_sb[:, u.parity, k, m * P:(m + 1) * P],
                                       lambda k: rows_t[:, u.parity, k, :])
                    step(gup_t, last)
                    step(gup_t, product(ps[:, 3, 0:CAP], lambda k: gu_sb[:, u.parity, k, 2 * P:3 * P],
                                        lambda k: rows_t[:, u.parity, k, :]))
                if d.exists():
                    wait_dma(pe, d_dn, d, 2)
                    wait(pe, gup_v, d, "h2")
                    for h in range(2):
                        if h == 0:
                            wait(pe, dwn_a, d.back(1), "y0")
                        else:
                            wait(pe, dwn_v, d.back(1), "y1")
                        half = slice(h * HS, (h + 1) * HS)
                        pe.matmul(ps[0:HS, 4 + h, :], h1[:, d.parity, half], dn_sb[:, d.parity, :],
                                  start=True, stop=False)
                        step(dwn_t, pe.matmul(ps[0:HS, 4 + h, :], h2[:, d.parity, half], dn2_sb[:, d.parity, :],
                                              start=False, stop=True))
                if g.exists():
                    wait_dma(pe, d_rows, g, 2)
                    for h in range(2):
                        if h == 0:
                            wait(pe, ffn_a, g.back(1), "rowsT0")
                        else:
                            wait(pe, ffn_v, g.back(1), "rowsT1")
                        for c in range(KC):
                            last = pe.transpose(ps[:, h, c * HS:(c + 1) * HS], rows[:, g.parity, h, c * P:(c + 1) * P],
                                                ident[0:HS, 0:HS])
                        step(ffn_t, last)
            expert_turns(pe, expert_turn)


def kernel(x, ctx_2048, mask_BxS2_bk0, L0_attn_wq, L0_attn_wk, L0_attn_wv, L0_attn_wout, L0_attn_lambda_q1,
           L0_attn_lambda_q2, L0_attn_lambda_k1, L0_attn_lambda_k2, L0_attn_subln_weight, L0_ffn_gate_weight,
           L0_ffn_gate_up_proj, L0_ffn_down_proj, L0_ffn_old_to_new):
    import concourse.bacc as bacc
    from concourse.bass_utils import run_bass_kernel_spmd

    f = lambda a: np.ascontiguousarray(np.asarray(a))

    def chunked(w):
        return w.T.reshape(w.shape[1] // P, P, w.shape[0]).transpose(1, 0, 2)

    def halves(w):
        return w.reshape(NH2, NF, 2, DM).transpose(0, 2, 1, 3).reshape(DM, DM)

    wq, wk = halves(f(L0_attn_wq)), halves(f(L0_attn_wk))
    gu = f(L0_ffn_gate_up_proj)
    g, u = gu[:, :INTER], gu[:, INTER:]
    gu = np.concatenate([g[:, :P], u[:, :P], g[:, P:], u[:, P:]], axis=1)
    gu = gu.transpose(0, 2, 1).reshape(E, KC, P, 2 * INTER).transpose(0, 2, 1, 3).reshape(E * P, KC, 2 * INTER)
    ctx = f(ctx_2048)
    angle = np.outer(np.arange(P), 1.0 / 10000.0 ** (np.arange(0, HALF, 2).astype(np.float64) / HALF))
    arrays = {
        "x": f(x).reshape(T, DM),
        "ctx_rows": ctx.reshape(NB * M, DM),
        "ctx_t": ctx.transpose(0, 2, 1).reshape(NB, KC, P, M).transpose(0, 2, 1, 3).reshape(NB * P, KC, M),
        "mask": f(mask_BxS2_bk0).reshape(NB * M),
        "weights": np.concatenate([chunked(w) for w in (wq, wk, f(L0_attn_wv), f(L0_attn_wout))]),
        "lambda_q1": f(L0_attn_lambda_q1),
        "lambda_q2": f(L0_attn_lambda_q2),
        "lambda_k1": f(L0_attn_lambda_k1),
        "lambda_k2": f(L0_attn_lambda_k2),
        "subln": f(L0_attn_subln_weight),
        "gate": f(L0_ffn_gate_weight),
        "gate_up": gu,
        "down_proj": f(L0_ffn_down_proj).transpose(0, 2, 1).reshape(E * INTER, DM),
        "old_to_new": f(L0_ffn_old_to_new),
        "cos_sin": np.stack([np.cos(angle), np.sin(angle)], axis=1).astype(np.float32),
    }
    arrays = {k: np.ascontiguousarray(v) for k, v in arrays.items()}
    nc = bacc.Bacc("TRN2", target_bir_lowering=False, num_devices=1)
    ap = {k: nc.dram_tensor(f"in_{k}", v.shape, mybir.dt.from_np(v.dtype), kind="ExternalInput").ap()
          for k, v in arrays.items()}
    out = nc.dram_tensor("layer_out", (T + CAP, DM), FP32, kind="ExternalOutput").ap()
    lambdas = [ap.pop(k) for k in ("lambda_q1", "lambda_q2", "lambda_k1", "lambda_k2")]
    decoder_layer(nc, lambdas=lambdas, out=out, **ap)
    result = run_bass_kernel_spmd(nc, [{f"in_{k}": v for k, v in arrays.items()}], core_ids=[0])
    return np.asarray(result.results[0]["layer_out"])[:T].reshape(NB, P, DM)
```

```python
import math
from contextlib import ExitStack

import numpy as np

import concourse.bass as bass
from concourse import mybir

FP32 = mybir.dt.float32
FP32R = mybir.dt.float32r
BF16 = mybir.dt.bfloat16
I32 = mybir.dt.int32
U8 = mybir.dt.uint8
ALU = mybir.AluOpType
ACT = mybir.ActivationFunctionType
AX = mybir.AxisListType

P = 128
NB = 32
DM = 512
KC = DM // P
NH2 = 8
HALF = 64
NF = HALF // 2
H = NH2 // 2
M = 128
NEXP = 128
E = 48
INTER = 192
CAP = 192
HS = CAP // 2
T = NB * P
EPS = 1e-5
INV_SCALING = float(P) ** 0.5
XSCALE = float(DM) ** -0.5
LAMBDA_INIT = 0.8 - 0.6 * math.exp(-0.3 * 12)
BIG = 1e30
ROW = DM + E
SLOTS = HS * 2 * E


class Batch:

    def __init__(self, pair, off, limit):
        self.pair, self.off, self.limit = pair, off, limit
        self.parity = off % 2
        self.half = pair + off // 2
        self.index = 2 * pair + off

    def exists(self):
        return not isinstance(self.pair, int) or 0 <= self.index < self.limit

    def first(self):
        return isinstance(self.pair, int) and self.index == 0

    def back(self, n):
        return Batch(self.pair, self.off - n, self.limit)


class Steps:

    def __init__(self, sem, names):
        self.sem, self.names = sem, names.split()

    def after(self, b, name):
        return len(self.names) * b.index + self.names.index(name) + 1


def moved(b, per_batch):
    return b.half * (16 * per_batch) + 16 * per_batch


def decoder_layer(nc, x, ctx_rows, ctx_t, mask, weights, lambdas, subln, gate, gate_up, down_proj,
                  old_to_new, cos_sin, out):
    xw = nc.dram_tensor("normed_rows_and_weights", (T + CAP, ROW), FP32, kind="Internal").ap()
    table = nc.dram_tensor("token_of_slot", (SLOTS, 1), I32, kind="Internal").ap()

    stack = ExitStack()
    with stack:
        def sb(name, shape, dt=FP32):
            return stack.enter_context(nc.sbuf_tensor(name, shape, dt))

        def sem(name):
            return stack.enter_context(nc.semaphore(name))

        w_raw = sb("w_raw", [P, 2, KC, DM])
        w_high = sb("w_high", [P, 4, KC, DM], FP32R)
        w_low = sb("w_low", [P, 4, KC, DM], FP32R)
        W_Q, W_K, W_V, W_OUT = range(4)
        gate_sb = sb("gate_sb", [NEXP, DM])
        gate_new = sb("gate_new", [P, KC, E])
        rope_tab = sb("rope_tab", [P, 2, NF])
        lam_in = sb("lam_in", [P, 4, HALF])
        lam_prod = sb("lam_prod", [P, 2, HALF])
        lam_sum = sb("lam_sum", [P, 2])
        lam_exp = sb("lam_exp", [P, 2])
        lam_gap = sb("lam_gap", [P, 1])
        neg_lam = sb("neg_lam", [P, 1])
        subln_sb = sb("subln_sb", [P, 1])
        mask_sb = sb("mask_sb", [P, NB * M], U8)
        valid = sb("valid", [P, NB])
        ident = sb("ident", [P, P])
        ones = sb("ones", [P, P])
        ones_bf = sb("ones_bf", [P, P], BF16)
        before_bf = sb("before_bf", [P, P], BF16)
        neg_half = sb("neg_half", [P, H])
        o2n_i = sb("o2n_i", [NEXP, 1], I32)
        o2n_f = sb("o2n_f", [NEXP, 1])
        expert_iota = sb("expert_iota", [P, E])
        is_new = sb("is_new", [NEXP, E])
        absent_bias = sb("absent_bias", [P, E])
        slot_base = sb("slot_base", [P, E])
        token_ids = sb("token_ids", [P, NB], I32)
        spare_ids = sb("spare_ids", [HS, E, 2], I32)

        x_ln = sb("x_ln", [P, 2, DM])
        qk_both = sb("qk_both", [P, 4 * DM])
        zeros = qk_both[0:HS, 0:2 * ROW]
        st1 = sb("st1", [P, 6])
        mv1 = sb("mv1", [P, 2])
        rstd1 = sb("rstd1", [P, 1])
        shift1 = sb("shift1", [P, 1])
        xn1 = sb("xn1", [P, 2, DM])
        xn1_high = sb("xn1_high", [P, KC, P], FP32R)
        xn1_low = sb("xn1_low", [P, KC, P], FP32R)
        qk_cos = qk_both[:, 0:2 * DM].rearrange("p (g r f) -> p g r f", r=2, f=NF)
        qk_sin = qk_both[:, 2 * DM:4 * DM].rearrange("p (g r f) -> p g r f", r=2, f=NF)
        qk_rot = sb("qk_rot", [P, 2 * NH2, 2, NF])
        q_t = sb("q_t", [P, H, P])
        k_t = sb("k_t", [P, H, P])
        v_sb = sb("v_sb", [P, 2, DM])
        neg_max = sb("neg_max", [P, 2, H])
        neg_max_s = sb("neg_max_s", [P, 2, H])
        probs = sb("probs", [P, 2, H, P])
        prob_sum = sb("prob_sum", [P, 2, H])
        coef = sb("coef", [P, 2, H])
        weighted = sb("weighted", [P, H, P])
        diff = sb("diff", [P, H, P])
        diff_t = sb("diff_t", [P, H, P])
        squares = sb("squares", [P, H, P])
        sq_sum = sb("sq_sum", [P, H])
        sq_mean = sb("sq_mean", [P, H])
        rstd_h = sb("rstd_h", [P, H])
        heads = sb("heads", [P, H, P])
        heads_t = sb("heads_t", [P, H, P])
        heads_high = sb("heads_high", [P, H, P], FP32R)
        heads_low = sb("heads_low", [P, H, P], FP32R)
        x_res = sb("x_res", [P, 2, DM])
        x1 = sb("x1", [P, 2, DM])
        st2 = sb("st2", [P, 6])
        mv2 = sb("mv2", [P, 2])
        rstd2 = sb("rstd2", [P, 1])
        xn2 = sb("xn2", [P, DM])
        xn2_t = sb("xn2_t", [P, KC, P])
        ctx_sb = sb("ctx_sb", [M, 2, DM])
        ctx_t_sb = sb("ctx_t_sb", [P, 2, KC, M])
        mask_bias = sb("mask_bias", [P, M])
        xscore_kept = sb("xscore_kept", [P, M])
        xscore = sb("xscore", [P, M])
        xneg_max = sb("xneg_max", [P, 1])
        xshifted = sb("xshifted", [P, M])
        xprobs = sb("xprobs", [P, M])
        xsum = sb("xsum", [P, 1])
        xprobs_t = sb("xprobs_t", [M, P])
        xinv = sb("xinv", [P, 1])
        xcoef = sb("xcoef", [P, 1])
        x2 = sb("x2", [P, 2, DM])
        st3 = sb("st3", [P, 6])
        mv3 = sb("mv3", [P, 2])
        rstd3 = sb("rstd3", [P, 1])
        row = sb("row", [P, 2, ROW])
        xn3_t = sb("xn3_t", [P, KC, P])
        logits = sb("logits", [P, E])
        top8 = sb("top8", [P, 8])
        rest = sb("rest", [P, E])
        chosen = sb("chosen", [P, E], BF16)
        lneg_max = sb("lneg_max", [P, 1])
        lexp = sb("lexp", [P, E])
        lexp_chosen = sb("lexp_chosen", [P, E])
        wsum = sb("wsum", [P, 1])
        winv = sb("winv", [P, 1])
        taken = sb("taken", [P, E])
        pos = sb("pos", [P, E])
        fits = sb("fits", [P, E])
        second_half = sb("second_half", [P, E])
        address = sb("address", [P, E])
        address2 = sb("address2", [P, E])
        key = sb("key", [P, E])
        slot8 = sb("slot8", [P, 8])
        no_slot = sb("no_slot", [P, 8])
        slot_idx = sb("slot_idx", [P, 2, 8], I32)
        token_id = sb("token_id", [P, 2], I32)

        gu_sb = sb("gu_sb", [P, 2, KC, 2 * INTER])
        dn_sb = sb("dn_sb", [P, 2, DM])
        dn2_sb = sb("dn2_sb", [P, 2, DM])
        assert 2 * (INTER - P) == P
        slot_table = sb("slot_table", [HS, E * 2], I32)
        gather_idx = sb("gather_idx", [HS, 2, 2], I32)
        scatter_idx = sb("scatter_idx", [HS, 2, 2], I32)
        rows = w_raw[0:HS, :, :, :].rearrange("p a c n -> p (a c n)")[:, 0:4 * ROW]\
            .rearrange("p (e h n) -> p e h n", e=2, h=2)
        weight_of = [sb("weight_even", [HS, 2]), sb("weight_odd", [HS, 2])]
        def split_buffers(w):
            flat = w[:, :, :, :].rearrange("p m c n -> p (m c n)")
            at = 0
            for parts, *shape in ((P, 2, KC, 2 * INTER), (P, 2, KC, CAP), (P, 2, 1, DM), (P, 2, 1, DM),
                                  (P, 2, 1, CAP), (P, 2, 1, CAP)):
                size = int(np.prod(shape))
                yield flat[0:parts, at:at + size].rearrange("p (e c n) -> p e c n", e=2, c=shape[1])
                at += size
        gu_high, rows_high, dn_high, dn2_high, h1_high, h2_both = split_buffers(w_high)
        gu_low, rows_low, dn_low, dn2_low, h1_low, _ = split_buffers(w_low)
        h2_high, h2_low = h2_both[0:INTER - P], h2_both[INTER - P:P]
        silu1 = sb("silu1", [P, CAP])
        silu2 = sb("silu2", [INTER - P, CAP])
        h1 = sb("h1", [P, CAP])
        h2 = sb("h2", [INTER - P, CAP])
        y = qk_both[0:HS, :].rearrange("p (e h n) -> p e h n", e=2, h=2)

        ps = stack.enter_context(nc.psum_tensor("ps", [P, 8, DM], FP32))
        bank_ta, bank_tb = ps[:, 0, :], ps[:, 1, :]
        banks_qk = ps[:, 2:4, :]
        bank_r = ps[:, 4, :]
        xscore_ps, logit_ps = bank_r[:, 0:M], bank_r[:, M:M + E]
        count_ps = bank_r[:, 2 * M:2 * M + 2 * E]
        bank_o = ps[:, 5, :]
        banks_s = ps[:, 6:8, :]
        bank_v = ps[:, 6, :]

        def blocks(bank):
            return bank.rearrange("p (c n) -> p c n", n=P)

        s_blank = sem("constants_filled")
        s_made = sem("constants_made")
        d_w = [sem(f"weights_loaded{m}") for m in range(4)]
        s_rope = sem("rope_table_loaded")
        s_split_a = sem("weights_high_made")
        s_split_v = sem("weights_low_made")
        s_late = sem("late_weights_loaded")
        once = Batch(0, 0, 1)
        setup_v = Steps(sem("setup_by_vector"), "prod sum old new gap lambda gate absent valid")
        setup_t = Steps(sem("setup_by_tensor"), "gate")
        setup_a = Steps(sem("setup_by_scalar"), "exp")
        s_spare = sem("spare_rows_written")
        d_xln = [sem("x_for_norm_loaded0"), sem("x_for_norm_loaded1")]
        d_xres = [sem("x_residual_loaded0"), sem("x_residual_loaded1")]
        d_ctx = [sem("context_loaded0"), sem("context_loaded1")]
        d_row = [sem("records_stored0"), sem("records_stored1")]
        d_x2 = [sem("residual_stored0"), sem("residual_stored1")]
        d_slot = [sem("slots_scattered0"), sem("slots_scattered1")]
        ln1 = Steps(sem("norm1_vector"), "stats aggr eps shift")
        ln1_p = Steps(sem("norm1_pool"), "rstd")
        ln1_a = Steps(sem("norm1_scalar"), "normed")
        prj_t = Steps(sem("project_tensor"), "xT q qk v qT kT")
        prj_a = Steps(sem("project_scalar"), "xT v qT kT")
        prj_v = Steps(sem("project_vector"), "low")
        rope = Steps(sem("rope_vector"), "cos sin real")
        rope_p = Steps(sem("rope_pool"), "imag")
        att_t = Steps(sem("attend_tensor"), "scores diffT pv")
        hds_t = Steps(sem("heads_tensor"), "headsT")
        hds_a = Steps(sem("heads_scalar"), "headsT high")
        att_o = Steps(sem("attend_tensor_project"), "proj")
        att_a = Steps(sem("attend_scalar"), "exp diffT square")
        att_v = Steps(sem("attend_vector"), "max negmax inv coef weighted diff sqmean heads")
        att_l = Steps(sem("attend_vector_low"), "low")
        att_p = Steps(sem("attend_pool"), "rstd")
        crs_v = Steps(sem("cross_vector"), "x1 stats aggr eps normed kept score max shifted")
        crs_b = Steps(sem("cross_vector_bias"), "bias")
        crs_p = Steps(sem("cross_pool"), "rstd")
        crs_t = Steps(sem("cross_tensor"), "xT scores probsT readout")
        crs_a = Steps(sem("cross_scalar"), "xT exp probsT")
        out_v = Steps(sem("readout_vector"), "inv coef x2 stats aggr eps normed")
        out_p = Steps(sem("readout_pool"), "rstd")
        rte_t = Steps(sem("route_tensor"), "xT logits counts")
        rte_a = Steps(sem("route_scalar"), "xT exp")
        rte_v = Steps(sem("route_vector"), "logits top8 rest chosen negmax pos taken")
        slt_v = Steps(sem("slots_vector"), "wsum winv fits weights half addr addr2 key slot8 none slots token")
        d_gu = [sem("gate_up_loaded0"), sem("gate_up_loaded1")]
        d_dn = [sem("down_loaded0"), sem("down_loaded1")]
        s_table = sem("slot_table_loaded")
        d_rows = [sem("rows_gathered0"), sem("rows_gathered1")]
        d_add = [sem("outputs_added0"), sem("outputs_added1")]
        gup_t = Steps(sem("gate_up_tensor"), "first second")
        gup_a = Steps(sem("gate_up_scalar"), "silu1 silu2 high1 high2")
        gup_v = Steps(sem("gate_up_vector"), "h1 h2 low1 low2")
        wgu_a = Steps(sem("gate_up_weights_scalar"), "high")
        wgu_v = Steps(sem("gate_up_weights_vector"), "low")
        wdn_a = Steps(sem("down_weights_scalar"), "high high2")
        wdn_v = Steps(sem("down_weights_vector"), "low low2")
        ffn_t = Steps(sem("rows_tensor"), "rowsT0 rowsT1")
        ffn_a = Steps(sem("rows_scalar"), "high0 high1")
        ffn_v = Steps(sem("rows_vector"), "low0 low1")
        ffn_w = Steps(sem("rows_vector_weight"), "weight")
        ffn_i = Steps(sem("rows_vector_index"), "index")
        dwn_t = Steps(sem("down_tensor"), "y0 y1")
        dwn_i = Steps(sem("down_vector_index"), "index")
        dwn_v = Steps(sem("down_vector"), "y1")
        dwn_a = Steps(sem("down_scalar"), "y0")

        def raw(m):
            if m == 2:
                return gu_sb[:, :, :, :].rearrange("p e c n -> p (e c n)")[:, 0:KC * DM]\
                    .rearrange("p (c n) -> p c n", c=KC)
            return w_raw[:, m % 3, :, :]

        block = stack.enter_context(nc.Block())

        SKEW = {"norm": 0, "project": 1, "attend": 2, "cross": 3, "route": 4, "slots": 5}
        PAIRS, FIRST, LAST = (NB + 6) // 2, 3, NB // 2

        def turns(eng, turn, after_first=None):
            def trip(pair):
                for j in range(2):
                    turn({k: Batch(pair, j - s, NB) for k, s in SKEW.items()})
                    if after_first and isinstance(pair, int) and 2 * pair + j == 0:
                        after_first()
            for pair in range(FIRST):
                trip(pair)
            with eng.Fori(FIRST, LAST) as pair:
                trip(pair)
            for pair in range(LAST, PAIRS):
                trip(pair)

        ESKEW = {"gather": 0, "turn": 1, "up": 2, "down": 3}
        EPAIRS, EFIRST, ELAST = (E + 4) // 2, 2, E // 2

        def expert_turns(eng, turn):
            def trip(pair):
                for j in range(2):
                    turn({k: Batch(pair, j - s, E) for k, s in ESKEW.items()})
            for pair in range(EFIRST):
                trip(pair)
            with eng.Fori(EFIRST, ELAST) as pair:
                trip(pair)
            for pair in range(ELAST, EPAIRS):
                trip(pair)

        s_paced = {nc.vector.engine: sem("vector_paced"), nc.gpsimd.engine: sem("pool_paced"),
                   nc.scalar.engine: sem("scalar_paced")}

        def settled(eng):
            eng.sem_inc(s_paced[eng.engine], 1)

        @block.sync
        def _(sp):
            def load_first():
                for m in range(3):
                    sp.dma_start(raw(m), weights[m * P:(m + 1) * P, :, :]).then_inc(d_w[m], 16)
                    if m == 0:
                        sp.dma_start(rope_tab[:, :, :], cos_sin).then_inc(s_rope, 16)

            def load_late():
                for n in range(4):
                    sp.dma_start(lam_in[:, n, :], lambdas[n].partition_broadcast(P)).then_inc(s_late, 16)
                sp.dma_start(subln_sb[:, :], subln.rearrange("(p o) -> p o", o=1)).then_inc(s_late, 16)
                sp.dma_start(o2n_i[:, :], old_to_new.rearrange("(p o) -> p o", o=1)).then_inc(s_late, 16)
                sp.dma_start(gate_sb[:, :], gate).then_inc(s_late, 16)
                sp.dma_start(mask_sb[:, :], mask.partition_broadcast(P)).then_inc(s_late, 16)
                sp.wait_ge(s_split_v, 1)
                sp.dma_start(raw(3), weights[3 * P:4 * P, :, :]).then_inc(d_w[3], 16)

            def turn(b):
                n, c, r, s = b["norm"], b["cross"], b["route"], b["slots"]
                if n.exists():
                    if n.back(2).exists():
                        sp.wait_ge(ln1_a.sem, ln1_a.after(n.back(2), "normed"))
                    sp.dma_start(x_ln[:, n.parity, :], x[bass.ds(n.index * P, P), :])\
                      .then_inc(d_xln[n.parity], 16)
                if c.exists():
                    if c.back(2).exists():
                        sp.wait_ge(crs_v.sem, crs_v.after(c.back(2), "x1"))
                    sp.dma_start(x_res[:, c.parity, :], x[bass.ds(c.index * P, P), :])\
                      .then_inc(d_xres[c.parity], 16)
                    if c.back(2).exists():
                        sp.wait_ge(crs_t.sem, crs_t.after(c.back(2), "readout"))
                    sp.dma_start(ctx_t_sb[:, c.parity, :, :], ctx_t[bass.ds(c.index * P, P), :, :])\
                      .then_inc(d_ctx[c.parity], 16)
                    sp.dma_start(ctx_sb[:, c.parity, :], ctx_rows[bass.ds(c.index * M, M), :])\
                      .then_inc(d_ctx[c.parity], 16)
                if r.exists():
                    sp.wait_ge(out_v.sem, out_v.after(r, "x2"))
                    sp.dma_start(out[bass.ds(r.index * P, P), :], x2[:, r.parity, :])\
                      .then_inc(d_x2[r.parity], 16)
                if s.exists():
                    sp.wait_ge(slt_v.sem, slt_v.after(s, "weights"))
                    sp.dma_start(xw[bass.ds(s.index * P, P), :], row[:, s.parity, :])\
                      .then_inc(d_row[s.parity], 16)
                if b["project"].first():
                    load_late()
            turns(sp, turn, load_first)

            def load_gate_up(e):
                if e.back(2).exists():
                    sp.wait_ge(wgu_v.sem, wgu_v.after(e.back(2), "low"))
                sp.dma_start(gu_sb[:, e.parity, :, :], gate_up[bass.ds(e.index * P, P), :, :])\
                  .then_inc(d_gu[e.parity], 16)

            def load_down(e):
                if e.back(2).exists():
                    sp.wait_ge(wdn_v.sem, wdn_v.after(e.back(2), "low2"))
                sp.dma_start(dn_sb[:, e.parity, :], down_proj[bass.ds(e.index * INTER, P), :])\
                  .then_inc(d_dn[e.parity], 16)
                for copy in range(2):
                    sp.dma_start(dn2_sb[copy * (INTER - P):(copy + 1) * (INTER - P), e.parity, :],
                                 down_proj[bass.ds(e.index * INTER + P, INTER - P), :])\
                      .then_inc(d_dn[e.parity], 16)

            sp.wait_ge(s_split_v, 3)
            for off in range(2):
                load_gate_up(Batch(0, off, E))
                load_down(Batch(0, off, E))
            for par in range(2):
                sp.wait_ge(d_slot[par], 16 * 8 * NB // 2)
            sp.dma_start(slot_table[:, :], table.rearrange("(p n) o -> p (n o)", p=HS)).then_inc(s_table, 16)
            load_gate_up(Batch(1, 0, E))
            with sp.Fori(1, E // 2 - 1) as pair:
                for off in range(2):
                    load_gate_up(Batch(pair, off + 1, E))
                    load_down(Batch(pair, off, E))
            load_gate_up(Batch(E // 2 - 1, 1, E))
            for off in range(2):
                load_down(Batch(E // 2 - 1, off, E))
            for par in range(2):
                sp.wait_ge(d_add[par], 16 * 2 * E // 2)

        @block.gpsimd
        def _(pool):
            pool.memset(ident[:, :], 0.0).then_inc(s_blank, 1)
            pool.memset(ones[:, :], 1.0)
            pool.memset(before_bf[:, :], 1.0).then_inc(s_blank, 1)
            pool.memset(neg_half[:, :], -0.5)
            pool.memset(zeros, 0.0)
            pool.iota(token_ids[:, :], [[P, NB]], base=0, channel_multiplier=1)
            pool.iota(spare_ids[:, :, :], [[0, E], [HS, 2]], base=T, channel_multiplier=1)
            pool.iota(expert_iota[:, :], [[1, E]], base=0, channel_multiplier=0,
                      allow_small_or_imprecise_dtypes=True)
            pool.iota(slot_base[:, :], [[2, E]], base=1, channel_multiplier=0,
                      allow_small_or_imprecise_dtypes=True)
            pool.memset(ones_bf[:, :], 1.0)
            pool.wait_ge(s_blank, 2)
            pool.affine_select(out=ident[:, :], in_=ident[:, :], compare_op=ALU.not_equal, fill=1.0, base=0,
                               pattern=[[-1, P]], channel_multiplier=1)
            pool.affine_select(out=before_bf[:, :], in_=before_bf[:, :], compare_op=ALU.is_gt, fill=0.0,
                               base=0, pattern=[[1, P]], channel_multiplier=-1).then_inc(s_made, 1)
            pool.wait_ge(s_made, 1)
            pool.dma_start(table.rearrange("(p n) o -> p (n o)", p=HS),
                           spare_ids[:, :, :].rearrange("p e h -> p (e h)")).then_inc(s_spare, 16)
            pool.dma_start(xw[T:T + CAP, :].rearrange("(p a) n -> p (a n)", a=2), zeros)\
                .then_inc(s_spare, 16)
            pool.dma_start(out[T:T + CAP, :].rearrange("(p a) n -> p (a n)", a=2), zeros[:, 0:2 * DM])\
                .then_inc(s_spare, 16)

            def turn(b):
                n, p, a, c, o, s = (b[k] for k in ("norm", "project", "attend", "cross", "route", "slots"))

                def scatter(k0):
                    for k in range(k0, k0 + 2):
                        pool.indirect_dma_start(
                            out=table, out_offset=bass.IndirectOffsetOnAxis(ap=slot_idx[:, s.parity, k:k + 1], axis=0),
                            in_=token_id[:, s.parity:s.parity + 1], in_offset=None,
                            bounds_check=SLOTS - 1, oob_is_err=False).then_inc(d_slot[s.parity], 16)

                for steps, ready, b_, rstd, mv in ((out_p, out_v, o, rstd3, mv3), (ln1_p, ln1, n, rstd1, mv1),
                                                   (crs_p, crs_v, c, rstd2, mv2)):
                    if b_.exists():
                        pool.wait_ge(ready.sem, ready.after(b_, "eps"))
                        pool.tensor_tensor(rstd[:, :], mv[:, 1:2], neg_half[:, 0:1], ALU.pow).then_inc(steps.sem, 1)
                if s.first():
                    pool.wait_ge(s_spare, 48)
                if s.exists():
                    pool.wait_ge(slt_v.sem, slt_v.after(s, "token"))
                    settled(pool)
                    scatter(0)
                    scatter(2)
                if p.exists():
                    pool.wait_ge(rope.sem, rope.after(p, "sin"))
                    if p.back(1).exists():
                        pool.wait_ge(prj_t.sem, prj_t.after(p.back(1), "kT"))
                    pool.tensor_tensor(qk_rot[:, :, 1, :], qk_cos[:, :, 1, :], qk_sin[:, :, 0, :], ALU.add)\
                        .then_inc(rope_p.sem, 1)
                if a.exists():
                    pool.wait_ge(att_v.sem, att_v.after(a, "sqmean"))
                    pool.tensor_tensor(rstd_h[:, :], sq_mean[:, :], neg_half[:, :], ALU.pow)\
                        .then_inc(att_p.sem, 1)
                if s.exists():
                    scatter(4)
                    scatter(6)
            turns(pool, turn)

            def gather(e):
                if e.exists():
                    pool.wait_ge(ffn_i.sem, ffn_i.after(e, "index"))
                if e.back(2).exists():
                    pool.wait_ge(ffn_t.sem, ffn_t.after(e.back(2), "rowsT1"))
                    pool.wait_ge(ffn_w.sem, ffn_w.after(e.back(2), "weight"))
                settled(pool)
                for h in range(2):
                    pool.indirect_dma_start(
                        out=rows[:, e.parity, h, :], out_offset=None, in_=xw,
                        in_offset=bass.IndirectOffsetOnAxis(ap=gather_idx[:, e.parity, h:h + 1], axis=0),
                        bounds_check=T + CAP - 1, oob_is_err=True).then_inc(d_rows[e.parity], 16)

            def expert_turn(b):
                g, d = b["gather"], b["down"]
                if g.exists():
                    gather(g)
                if d.exists():
                    if d.back(1).exists():
                        pool.wait_ge(d_add[d.back(1).parity], moved(d.back(1), 2))
                    pool.wait_ge(dwn_a.sem, dwn_a.after(d, "y0"))
                    pool.wait_ge(dwn_v.sem, dwn_v.after(d, "y1"))
                    pool.wait_ge(dwn_i.sem, dwn_i.after(d, "index"))
                    settled(pool)
                    for h in range(2):
                        pool.indirect_dma_start(
                            out=out, out_offset=bass.IndirectOffsetOnAxis(ap=scatter_idx[:, d.parity, h:h + 1], axis=0),
                            in_=y[:, d.parity, h, :], in_offset=None,
                            bounds_check=T + CAP - 1, oob_is_err=True,
                            compute_op=ALU.add).then_inc(d_add[d.parity], 16)
            for par in range(2):
                pool.wait_ge(d_row[par], 16 * NB // 2)
                pool.wait_ge(d_x2[par], 16 * NB // 2)
            expert_turns(pool, expert_turn)

        @block.scalar
        def _(act):
            def copy(dst, src, steps, scale=None):
                if scale is None:
                    act.activation(dst, src, ACT.Copy).then_inc(steps.sem, 1)
                else:
                    act.activation(dst, src, ACT.Copy, scale=scale).then_inc(steps.sem, 1)

            def split(m):
                act.wait_ge(d_w[m], 16)
                act.activation(w_high[:, m, :, :], raw(m), ACT.Copy).then_inc(s_split_a, 1)

            def split_first():
                for m in range(3):
                    split(m)

            def turn(b):
                n, p, a, c, r = (b[k] for k in ("norm", "project", "attend", "cross", "route"))
                if p.exists():
                    act.wait_ge(prj_t.sem, prj_t.after(p, "xT"))
                    if p.back(1).exists():
                        act.wait_ge(prj_t.sem, prj_t.after(p.back(1), "v"))
                        act.wait_ge(prj_v.sem, prj_v.after(p.back(1), "low"))
                    copy(xn1_high[:, :, :], blocks(bank_ta), prj_a)
                if c.exists():
                    act.wait_ge(hds_t.sem, hds_t.after(c, "headsT"))
                    if c.back(1).exists():
                        act.wait_ge(att_l.sem, att_l.after(c.back(1), "low"))
                    copy(heads_t[:, :, :], blocks(bank_tb), hds_a, scale=subln_sb[:, :])
                    act.wait_ge(hds_a.sem, hds_a.after(c, "headsT"))
                    if c.back(1).exists():
                        act.wait_ge(att_o.sem, att_o.after(c.back(1), "proj"))
                    copy(heads_high[:, :, :], heads_t[:, :, :], hds_a)
                if a.exists():
                    act.wait_ge(att_v.sem, att_v.after(a, "negmax"))
                    if a.back(1).exists():
                        act.wait_ge(att_v.sem, att_v.after(a.back(1), "diff"))
                    for s in range(2):
                        for h in range(H):
                            last = act.activation(probs[:, s, h, :], blocks(banks_s[:, s, :])[:, h, :], ACT.Exp,
                                                  bias=neg_max_s[:, s, h:h + 1], scale=INV_SCALING,
                                                  accum_out=prob_sum[:, s, h:h + 1])
                    last.then_inc(att_a.sem, 1)
                if r.exists():
                    act.wait_ge(rte_t.sem, rte_t.after(r, "xT"))
                    copy(xn3_t[:, :, :], blocks(bank_tb), rte_a)
                if n.exists():
                    act.wait_ge(ln1.sem, ln1.after(n, "shift"))
                    if n.back(2).exists():
                        act.wait_ge(prj_t.sem, prj_t.after(n.back(2), "xT"))
                    act.activation(xn1[:, n.parity, :], x_ln[:, n.parity, :], ACT.Identity, bias=shift1[:, :],
                                   scale=rstd1[:, :]).then_inc(ln1_a.sem, 1)
                if c.exists():
                    act.wait_ge(crs_t.sem, crs_t.after(c, "xT"))
                    copy(xn2_t[:, :, :], blocks(bank_ta), crs_a)
                if a.exists():
                    act.wait_ge(att_t.sem, att_t.after(a, "diffT"))
                    copy(diff_t[:, :, :], blocks(bank_tb), att_a)
                if c.exists():
                    act.wait_ge(crs_v.sem, crs_v.after(c, "shifted"))
                    if c.back(1).exists():
                        act.wait_ge(out_v.sem, out_v.after(c.back(1), "inv"))
                    act.activation(xprobs[:, :], xshifted[:, :], ACT.Exp, scale=XSCALE,
                                   accum_out=xsum[:, :]).then_inc(crs_a.sem, 1)
                if a.exists():
                    act.wait_ge(att_t.sem, att_t.after(a, "pv"))
                    if a.back(1).exists():
                        act.wait_ge(att_v.sem, att_v.after(a.back(1), "sqmean"))
                    for h in range(H):
                        last = act.activation(squares[:, h, :], blocks(bank_o)[:, h, :], ACT.Square,
                                              accum_out=sq_sum[:, h:h + 1])
                    last.then_inc(att_a.sem, 1)
                if c.exists():
                    act.wait_ge(crs_t.sem, crs_t.after(c, "probsT"))
                    copy(xprobs_t[:, :], bank_ta[:, 0:P], crs_a)
                if r.exists():
                    act.wait_ge(rte_v.sem, rte_v.after(r, "negmax"))
                    if r.back(1).exists():
                        act.wait_ge(slt_v.sem, slt_v.after(r.back(1), "wsum"))
                    act.activation(lexp[:, :], logits[:, :], ACT.Exp, bias=lneg_max[:, :])\
                        .then_inc(rte_a.sem, 1)
                if p.exists():
                    act.wait_ge(prj_t.sem, prj_t.after(p, "v"))
                    if p.back(2).exists():
                        act.wait_ge(att_t.sem, att_t.after(p.back(2), "pv"))
                    copy(v_sb[:, p.parity, :], bank_v, prj_a)
                if p.exists():
                    act.wait_ge(prj_t.sem, prj_t.after(p, "qT"))
                    if p.back(1).exists():
                        act.wait_ge(att_t.sem, att_t.after(p.back(1), "scores"))
                    copy(q_t[:, :, :], blocks(bank_tb), prj_a)
                    act.wait_ge(prj_t.sem, prj_t.after(p, "kT"))
                    copy(k_t[:, :, :], blocks(bank_ta), prj_a)
                if p.first():
                    act.wait_ge(s_late, 16 * 8)
                    act.wait_ge(setup_v.sem, setup_v.after(once, "sum"))
                    act.activation(lam_exp[:, :], lam_sum[:, :], ACT.Exp).then_inc(setup_a.sem, 1)
                if a.first():
                    split(3)
            turns(act, turn, split_first)

            def expert_turn(b):
                t, u, d = b["turn"], b["up"], b["down"]
                if t.exists():
                    act.wait_ge(d_gu[t.parity], moved(t, 1))
                    if t.back(2).exists():
                        act.wait_ge(gup_t.sem, gup_t.after(t.back(2), "second"))
                    copy(gu_high[:, t.parity, :, :], gu_sb[:, t.parity, :, :], wgu_a)
                if u.exists():
                    act.wait_ge(gup_t.sem, gup_t.after(u, "first"))
                    if u.back(1).exists():
                        act.wait_ge(gup_v.sem, gup_v.after(u.back(1), "h2"))
                    act.activation(silu1[:, :], ps[:, 2, 0:CAP], ACT.Silu).then_inc(gup_a.sem, 1)
                    act.wait_ge(gup_t.sem, gup_t.after(u, "second"))
                    act.activation(silu2[:, :], ps[0:INTER - P, 3, 0:CAP], ACT.Silu).then_inc(gup_a.sem, 1)
                if t.exists():
                    for h in range(2):
                        act.wait_ge(ffn_t.sem, ffn_t.after(t, f"rowsT{h}"))
                        if t.back(2).exists():
                            act.wait_ge(gup_t.sem, gup_t.after(t.back(2), "second"))
                        copy(rows_high[:, t.parity, :, h * HS:(h + 1) * HS],
                             ps[:, h, 0:KC * HS].rearrange("p (c n) -> p c n", c=KC), ffn_a)
                if u.exists():
                    if u.back(2).exists():
                        act.wait_ge(dwn_t.sem, dwn_t.after(u.back(2), "y1"))
                    for h, dst, name in ((h1, h1_high, "h1"), (h2, h2_high, "h2")):
                        act.wait_ge(gup_v.sem, gup_v.after(u, name))
                        copy(dst[:, u.parity, 0, :], h[:, :], gup_a)
                if d.exists():
                    act.wait_ge(dwn_t.sem, dwn_t.after(d, "y0"))
                    act.wait_ge(ffn_w.sem, ffn_w.after(d, "weight"))
                    if d.back(2).exists():
                        act.wait_ge(d_add[d.back(2).parity], moved(d.back(2), 2))
                    copy(y[:, d.parity, 0, :], ps[0:HS, 4, :], dwn_a, scale=weight_of[d.parity][:, 0:1])
                if u.exists():
                    act.wait_ge(d_dn[u.parity], moved(u, 3))
                    if u.back(2).exists():
                        act.wait_ge(dwn_t.sem, dwn_t.after(u.back(2), "y1"))
                    copy(dn_high[:, u.parity, 0, :], dn_sb[:, u.parity, :], wdn_a)
                    copy(dn2_high[:, u.parity, 0, :], dn2_sb[:, u.parity, :], wdn_a)
            expert_turns(act, expert_turn)

        @block.vector
        def _(dve):
            def split(m):
                dve.wait_ge(s_split_a, m + 1)
                dve.tensor_tensor(w_low[:, m, :, :], raw(m), w_high[:, m, :, :].bitcast(FP32), ALU.subtract)\
                    .then_inc(s_split_v, 1)

            def setup_attention():
                dve.wait_ge(s_late, 16 * 8)
                dve.tensor_tensor(lam_prod[:, :, :], lam_in[:, 0:2, :], lam_in[:, 2:4, :], ALU.mult).then_inc(setup_v.sem, 1)
                dve.wait_ge(setup_v.sem, setup_v.after(once, "prod"))
                dve.reduce_sum(lam_sum[:, :], lam_prod[:, :, :], AX.X).then_inc(setup_v.sem, 1)
                dve.tensor_copy(o2n_f[:, :], o2n_i[:, :]).then_inc(setup_v.sem, 1)
                dve.wait_ge(setup_v.sem, setup_v.after(once, "old"))
                dve.wait_ge(s_made, 1)
                dve.tensor_scalar(is_new[:, :], expert_iota[:, :], o2n_f[:, :], None, ALU.is_equal).then_inc(setup_v.sem, 1)
                dve.wait_ge(setup_a.sem, setup_a.after(once, "exp"))
                dve.tensor_tensor(lam_gap[:, :], lam_exp[:, 1:2], lam_exp[:, 0:1], ALU.subtract).then_inc(setup_v.sem, 1)
                dve.wait_ge(setup_v.sem, setup_v.after(once, "gap"))
                dve.tensor_scalar_add(neg_lam[:, :], lam_gap[:, :], -LAMBDA_INIT).then_inc(setup_v.sem, 1)
                dve.wait_ge(setup_v.sem, setup_v.after(once, "lambda"))

            def setup_router():
                dve.memset(taken[:, :], 0.0)
                dve.wait_ge(setup_t.sem, setup_t.after(once, "gate"))
                dve.tensor_copy(gate_new[:, :, :], ps[:, 7, 0:KC * E]
                                              .rearrange("p (c e) -> p c e", c=KC)).then_inc(setup_v.sem, 1)
                dve.tensor_scalar(absent_bias[:, :], ps[:, 7, KC * E:(KC + 1) * E], -1.0, BIG,
                                                ALU.add, ALU.mult).then_inc(setup_v.sem, 1)
                dve.reduce_max(valid[:, :], mask_sb[:, :].rearrange("p (b m) -> p b m", m=M), AX.X).then_inc(setup_v.sem, 1)
                dve.wait_ge(setup_v.sem, setup_v.after(once, "valid"))

            def turn(b):
                n, p, a, c, r, s = (b[k] for k in ("norm", "project", "attend", "cross", "route", "slots"))
                if r.exists():
                    dve.wait_ge(crs_a.sem, crs_a.after(r, "exp"))
                    dve.reciprocal(xinv[:, :], xsum[:, :]).then_inc(out_v.sem, 1)
                if s.exists():
                    dve.wait_ge(rte_a.sem, rte_a.after(s, "exp"))
                    dve.scalar_tensor_tensor(lexp_chosen[:, :], lexp[:, :], 1.0, chosen[:, :],
                                                         ALU.mult, ALU.mult, accum_out=wsum[:, :]).then_inc(slt_v.sem, 1)
                if r.exists():
                    dve.wait_ge(out_v.sem, out_v.after(r, "inv"))
                    dve.tensor_scalar(xcoef[:, :], valid[:, bass.ds(r.index, 1)], xinv[:, :], None,
                                                  ALU.mult).then_inc(out_v.sem, 1)
                if s.exists():
                    dve.wait_ge(slt_v.sem, slt_v.after(s, "wsum"))
                    dve.reciprocal(winv[:, :], wsum[:, :]).then_inc(slt_v.sem, 1)
                    dve.scalar_tensor_tensor(fits[:, :], pos[:, :], float(CAP), chosen[:, :],
                                                         ALU.is_lt, ALU.mult).then_inc(slt_v.sem, 1)
                if r.exists():
                    dve.wait_ge(out_v.sem, out_v.after(r, "coef"))
                    dve.wait_ge(crs_t.sem, crs_t.after(r, "readout"))
                    if r.back(2).exists():
                        dve.wait_ge(d_x2[r.back(2).parity], moved(r.back(2), 1))
                    dve.scalar_tensor_tensor(x2[:, r.parity, :], bank_r, xcoef[:, :], x1[:, r.parity, :],
                                                         ALU.mult, ALU.add).then_inc(out_v.sem, 1)
                if s.exists():
                    dve.wait_ge(slt_v.sem, slt_v.after(s, "winv"))
                    dve.tensor_scalar(row[:, s.parity, DM:ROW], lexp_chosen[:, :], winv[:, :], None,
                                                  ALU.mult).then_inc(slt_v.sem, 1)
                    dve.tensor_scalar(second_half[:, :], pos[:, :], float(HS), float(1 - 2 * E * HS),
                                                  ALU.is_ge, ALU.mult).then_inc(slt_v.sem, 1)
                    dve.scalar_tensor_tensor(address[:, :], pos[:, :], float(2 * E), slot_base[:, :],
                                                         ALU.mult, ALU.add).then_inc(slt_v.sem, 1)
                if p.exists():
                    dve.wait_ge(prj_a.sem, prj_a.after(p, "xT"))
                    if p.back(1).exists():
                        dve.wait_ge(prj_t.sem, prj_t.after(p.back(1), "v"))
                    dve.tensor_tensor(xn1_low[:, :, :], blocks(bank_ta), xn1_high[:, :, :].bitcast(FP32),
                                                  ALU.subtract).then_inc(prj_v.sem, 1)
                if s.exists():
                    dve.wait_ge(slt_v.sem, slt_v.after(s, "addr"))
                    dve.tensor_tensor(address2[:, :], address[:, :], second_half[:, :], ALU.add).then_inc(slt_v.sem, 1)
                if r.exists():
                    dve.wait_ge(out_v.sem, out_v.after(r, "x2"))
                    dve.bn_stats(st3[:, :], x2[:, r.parity, :]).then_inc(out_v.sem, 1)
                if s.exists():
                    dve.wait_ge(slt_v.sem, slt_v.after(s, "addr2"))
                    dve.tensor_tensor(key[:, :], address2[:, :], fits[:, :], ALU.mult).then_inc(slt_v.sem, 1)
                if a.exists():
                    dve.wait_ge(att_t.sem, att_t.after(a, "scores"))
                    if a.back(1).exists():
                        dve.wait_ge(att_a.sem, att_a.after(a.back(1), "exp"))
                    dve.tensor_reduce(neg_max[:, :, :], banks_s.rearrange("p s (h n) -> p s h n", n=P),
                                                  AX.X, ALU.max, negate=True).then_inc(att_v.sem, 1)
                if r.exists():
                    dve.wait_ge(out_v.sem, out_v.after(r, "stats"))
                    settled(dve)
                    dve.bn_aggr(mv3[:, :], st3[:, :]).then_inc(out_v.sem, 1)
                if a.exists():
                    dve.wait_ge(att_v.sem, att_v.after(a, "max"))
                    dve.tensor_scalar_mul(neg_max_s[:, :, :], neg_max[:, :, :], INV_SCALING).then_inc(att_v.sem, 1)
                if r.exists():
                    dve.wait_ge(out_v.sem, out_v.after(r, "aggr"))
                    dve.tensor_scalar_add(mv3[:, 1:2], mv3[:, 1:2], EPS).then_inc(out_v.sem, 1)
                if c.exists():
                    dve.wait_ge(hds_a.sem, hds_a.after(c, "high"))
                    if c.back(1).exists():
                        dve.wait_ge(att_o.sem, att_o.after(c.back(1), "proj"))
                    dve.tensor_tensor(heads_low[:, :, :], heads_t[:, :, :],
                                                  heads_high[:, :, :].bitcast(FP32), ALU.subtract).then_inc(att_l.sem, 1)
                if r.exists():
                    dve.wait_ge(out_p.sem, out_p.after(r, "rstd"))
                    if r.back(2).exists():
                        dve.wait_ge(d_row[r.back(2).parity], moved(r.back(2), 1))
                    dve.tensor_scalar(row[:, r.parity, 0:DM], x2[:, r.parity, :], mv3[:, 0:1], rstd3[:, :],
                                                  ALU.subtract, ALU.mult).then_inc(out_v.sem, 1)
                if s.exists():
                    dve.wait_ge(slt_v.sem, slt_v.after(s, "key"))
                    settled(dve)
                    dve.max(slot8[:, :], key[:, :]).then_inc(slt_v.sem, 1)
                if n.exists():
                    dve.wait_ge(d_xln[n.parity], moved(n, 1))
                    if n.back(1).exists():
                        dve.wait_ge(ln1_a.sem, ln1_a.after(n.back(1), "normed"))
                    dve.bn_stats(st1[:, :], x_ln[:, n.parity, :]).then_inc(ln1.sem, 1)
                if s.exists():
                    dve.wait_ge(slt_v.sem, slt_v.after(s, "slot8"))
                    dve.tensor_scalar(no_slot[:, :], slot8[:, :], 0.0, 1e6, ALU.is_equal, ALU.mult).then_inc(slt_v.sem, 1)
                if n.exists():
                    dve.wait_ge(ln1.sem, ln1.after(n, "stats"))
                    settled(dve)
                    dve.bn_aggr(mv1[:, :], st1[:, :]).then_inc(ln1.sem, 1)
                if s.exists():
                    dve.wait_ge(slt_v.sem, slt_v.after(s, "none"))
                    if s.back(2).exists():
                        dve.wait_ge(d_slot[s.back(2).parity], moved(s.back(2), 8))
                    dve.scalar_tensor_tensor(slot_idx[:, s.parity, :], no_slot[:, :], -1.0, slot8[:, :],
                                                         ALU.add, ALU.add).then_inc(slt_v.sem, 1)
                if n.exists():
                    dve.wait_ge(ln1.sem, ln1.after(n, "aggr"))
                    dve.tensor_scalar_add(mv1[:, 1:2], mv1[:, 1:2], EPS).then_inc(ln1.sem, 1)
                if c.exists():
                    dve.wait_ge(d_xres[c.parity], moved(c, 1))
                    dve.wait_ge(att_o.sem, att_o.after(c, "proj"))
                    dve.tensor_tensor(x1[:, c.parity, :], bank_o, x_res[:, c.parity, :], ALU.add).then_inc(crs_v.sem, 1)
                if a.exists():
                    dve.wait_ge(att_a.sem, att_a.after(a, "exp"))
                    dve.reciprocal(coef[:, :, :], prob_sum[:, :, :]).then_inc(att_v.sem, 1)
                if c.exists():
                    dve.wait_ge(crs_v.sem, crs_v.after(c, "x1"))
                    dve.bn_stats(st2[:, :], x1[:, c.parity, :]).then_inc(crs_v.sem, 1)
                if a.exists():
                    dve.wait_ge(att_v.sem, att_v.after(a, "inv"))
                    dve.tensor_scalar(coef[:, 1, :], coef[:, 1, :], neg_lam[:, :], None, ALU.mult).then_inc(att_v.sem, 1)
                if n.exists():
                    dve.wait_ge(ln1_p.sem, ln1_p.after(n, "rstd"))
                    dve.scalar_tensor_tensor(shift1[:, :], mv1[:, 0:1], -1.0, rstd1[:, :],
                                                       ALU.mult, ALU.mult).then_inc(ln1.sem, 1)
                if c.exists():
                    dve.wait_ge(crs_v.sem, crs_v.after(c, "stats"))
                    settled(dve)
                    dve.bn_aggr(mv2[:, :], st2[:, :]).then_inc(crs_v.sem, 1)
                if s.exists():
                    dve.tensor_scalar_add(token_id[:, s.parity:s.parity + 1],
                                                      token_ids[:, bass.ds(s.index, 1)], 0.0).then_inc(slt_v.sem, 1)
                if c.exists():
                    mask_row = mask_sb[:, bass.ds(c.index * M, M)]
                    dve.wait_ge(crs_v.sem, crs_v.after(c, "aggr"))
                    dve.tensor_scalar_add(mv2[:, 1:2], mv2[:, 1:2], EPS).then_inc(crs_v.sem, 1)
                if a.exists():
                    dve.wait_ge(att_v.sem, att_v.after(a, "coef"))
                    dve.tensor_tensor(weighted[:, :, :], probs[:, 1, :, :],
                                                  coef[:, 1, :].unsqueeze(2).to_broadcast([P, H, P]), ALU.mult).then_inc(att_v.sem, 1)
                if c.exists():
                    if c.back(1).exists():
                        dve.wait_ge(crs_v.sem, crs_v.after(c.back(1), "score"))
                    dve.tensor_scalar(mask_bias[:, :], mask_row, -1.0, BIG, ALU.add, ALU.mult).then_inc(crs_b.sem, 1)
                    dve.wait_ge(crs_p.sem, crs_p.after(c, "rstd"))
                    if c.back(1).exists():
                        dve.wait_ge(crs_t.sem, crs_t.after(c.back(1), "xT"))
                    dve.tensor_scalar(xn2[:, :], x1[:, c.parity, :], mv2[:, 0:1], rstd2[:, :],
                                                  ALU.subtract, ALU.mult).then_inc(crs_v.sem, 1)
                if a.exists():
                    dve.wait_ge(att_v.sem, att_v.after(a, "weighted"))
                    if a.back(1).exists():
                        dve.wait_ge(att_t.sem, att_t.after(a.back(1), "diffT"))
                    for h in range(H):
                        last = dve.scalar_tensor_tensor(diff[:, h, :], probs[:, 0, h, :], coef[:, 0, h:h + 1],
                                                        weighted[:, h, :], ALU.mult, ALU.add)
                    last.then_inc(att_v.sem, 1)
                def rotary(buf, i):
                    qk = banks_qk.rearrange("p a (g f) -> p (a g) f", f=NF)
                    dve.tensor_tensor(
                        buf[:, :, :, :].rearrange("p g r f -> p (g r) f"), qk,
                        rope_tab[:, i:i + 1, :].to_broadcast([P, 4 * NH2, NF]), ALU.mult).then_inc(rope.sem, 1)
                if p.first():
                    split(1)
                    split(2)
                    dve.wait_ge(s_rope, 16)
                    dve.wait_ge(s_spare, 48)
                if p.exists():
                    dve.wait_ge(prj_t.sem, prj_t.after(p, "qk"))
                    if p.back(1).exists():
                        dve.wait_ge(rope_p.sem, rope_p.after(p.back(1), "imag"))
                    rotary(qk_cos, 0)
                if r.exists():
                    dve.wait_ge(rte_t.sem, rte_t.after(r, "logits"))
                    if c.exists():
                        dve.wait_ge(crs_t.sem, crs_t.after(c, "scores"))
                    if r.back(1).exists():
                        dve.wait_ge(rte_a.sem, rte_a.after(r.back(1), "exp"))
                    dve.tensor_tensor(logits[:, :], logit_ps, absent_bias[:, :], ALU.add).then_inc(rte_v.sem, 1)
                if c.exists():
                    dve.wait_ge(crs_t.sem, crs_t.after(c, "scores"))
                    dve.tensor_tensor(xscore_kept[:, :], xscore_ps, mask_row, ALU.mult).then_inc(crs_v.sem, 1)
                if r.exists():
                    dve.wait_ge(rte_v.sem, rte_v.after(r, "logits"))
                    settled(dve)
                    dve.max(top8[:, :], logits[:, :]).then_inc(rte_v.sem, 1)
                if c.exists():
                    dve.wait_ge(crs_v.sem, crs_v.after(c, "kept"))
                    dve.wait_ge(crs_b.sem, crs_b.after(c, "bias"))
                    dve.tensor_tensor(xscore[:, :], xscore_kept[:, :], mask_bias[:, :], ALU.add).then_inc(crs_v.sem, 1)
                if r.exists():
                    dve.wait_ge(rte_v.sem, rte_v.after(r, "top8"))
                    settled(dve)
                    dve.match_replace(rest[:, :], top8[:, :], logits[:, :], -3e38).then_inc(rte_v.sem, 1)
                if c.exists():
                    dve.wait_ge(crs_v.sem, crs_v.after(c, "score"))
                    dve.tensor_reduce(xneg_max[:, :], xscore[:, :], AX.X, ALU.max, negate=True).then_inc(crs_v.sem, 1)
                if r.exists():
                    dve.wait_ge(rte_v.sem, rte_v.after(r, "rest"))
                    dve.tensor_tensor(chosen[:, :], rest[:, :], logits[:, :], ALU.is_lt).then_inc(rte_v.sem, 1)
                if c.exists():
                    dve.wait_ge(crs_v.sem, crs_v.after(c, "max"))
                    if c.back(1).exists():
                        dve.wait_ge(crs_a.sem, crs_a.after(c.back(1), "exp"))
                    dve.tensor_scalar(xshifted[:, :], xscore[:, :], xneg_max[:, :], None, ALU.add).then_inc(crs_v.sem, 1)
                if r.exists():
                    dve.tensor_scalar_mul(lneg_max[:, :], top8[:, 0:1], -1.0).then_inc(rte_v.sem, 1)
                if p.exists():
                    rotary(qk_sin, 1)
                if p.exists():
                    dve.wait_ge(rope.sem, rope.after(p, "sin"))
                    if p.back(1).exists():
                        dve.wait_ge(prj_t.sem, prj_t.after(p.back(1), "kT"))
                    dve.tensor_tensor(qk_rot[:, :, 0, :], qk_cos[:, :, 0, :], qk_sin[:, :, 1, :],
                                                 ALU.subtract).then_inc(rope.sem, 1)
                if a.exists():
                    dve.wait_ge(att_a.sem, att_a.after(a, "square"))
                    dve.tensor_scalar(sq_mean[:, :], sq_sum[:, :], 1.0 / P, EPS, ALU.mult, ALU.add).then_inc(att_v.sem, 1)
                if r.exists():
                    dve.wait_ge(rte_t.sem, rte_t.after(r, "counts"))
                    dve.tensor_tensor(pos[:, :], count_ps[:, 0:E], taken[:, :], ALU.add).then_inc(rte_v.sem, 1)
                    dve.wait_ge(rte_v.sem, rte_v.after(r, "pos"))
                    dve.tensor_tensor(taken[:, :], count_ps[:, E:2 * E], taken[:, :], ALU.add).then_inc(rte_v.sem, 1)
                if a.exists():
                    dve.wait_ge(att_p.sem, att_p.after(a, "rstd"))
                    if a.back(1).exists():
                        dve.wait_ge(hds_t.sem, hds_t.after(a.back(1), "headsT"))
                    dve.tensor_tensor(heads[:, :, :], blocks(bank_o),
                                                  rstd_h[:, :].unsqueeze(2).to_broadcast([P, H, P]), ALU.mult).then_inc(att_v.sem, 1)
                if p.first():
                    setup_attention()
                if a.first():
                    split(3)
                if c.first():
                    setup_router()
            turns(dve, turn, lambda: split(0))

            dve.wait_ge(s_table, 16)

            def left_by(dst, src, high):
                return dve.tensor_tensor(dst, src, high.bitcast(FP32), ALU.subtract)

            def expert_turn(b):
                g, t, u, d = b["gather"], b["turn"], b["up"], b["down"]
                if g.exists():
                    if g.back(2).exists():
                        dve.wait_ge(d_rows[g.back(2).parity], moved(g.back(2), 2))
                    dve.tensor_scalar_add(gather_idx[:, g.parity, :],
                                                      slot_table[:, bass.ds(2 * g.index, 2)], 0.0).then_inc(ffn_i.sem, 1)
                if t.exists():
                    dve.wait_ge(wgu_a.sem, wgu_a.after(t, "high"))
                    if t.back(2).exists():
                        dve.wait_ge(gup_t.sem, gup_t.after(t.back(2), "second"))
                    left_by(gu_low[:, t.parity, :, :], gu_sb[:, t.parity, :, :],
                                        gu_high[:, t.parity, :, :]).then_inc(wgu_v.sem, 1)
                if d.exists():
                    if d.back(2).exists():
                        dve.wait_ge(d_add[d.back(2).parity], moved(d.back(2), 2))
                    dve.tensor_scalar_add(scatter_idx[:, d.parity, :],
                                                      slot_table[:, bass.ds(2 * d.index, 2)], 0.0).then_inc(dwn_i.sem, 1)
                if u.exists():
                    dve.wait_ge(gup_a.sem, gup_a.after(u, "silu1"))
                    if u.back(1).exists():
                        dve.wait_ge(gup_v.sem, gup_v.after(u.back(1), "low2"))
                    dve.tensor_tensor(h1[:, :], silu1[:, :], ps[:, 2, CAP:2 * CAP], ALU.mult).then_inc(gup_v.sem, 1)
                    dve.wait_ge(gup_a.sem, gup_a.after(u, "silu2"))
                    dve.tensor_tensor(h2[:, :], silu2[:, :], ps[INTER - P:P, 3, 0:CAP], ALU.mult).then_inc(gup_v.sem, 1)
                if t.exists():
                    for h in range(2):
                        dve.wait_ge(ffn_a.sem, ffn_a.after(t, f"high{h}"))
                        if t.back(2).exists():
                            dve.wait_ge(gup_t.sem, gup_t.after(t.back(2), "second"))
                        half = slice(h * HS, (h + 1) * HS)
                        left_by(rows_low[:, t.parity, :, half],
                                            ps[:, h, 0:KC * HS].rearrange("p (c n) -> p c n", c=KC),
                                            rows_high[:, t.parity, :, half]).then_inc(ffn_v.sem, 1)
                if u.exists():
                    if u.back(2).exists():
                        dve.wait_ge(dwn_t.sem, dwn_t.after(u.back(2), "y1"))
                    dve.wait_ge(gup_a.sem, gup_a.after(u, "high1"))
                    left_by(h1_low[:, u.parity, 0, :], h1[:, :], h1_high[:, u.parity, 0, :]).then_inc(gup_v.sem, 1)
                    dve.wait_ge(gup_a.sem, gup_a.after(u, "high2"))
                    left_by(h2_low[:, u.parity, 0, :], h2[:, :], h2_high[:, u.parity, 0, :]).then_inc(gup_v.sem, 1)
                if d.exists():
                    dve.wait_ge(dwn_t.sem, dwn_t.after(d, "y1"))
                    dve.wait_ge(ffn_w.sem, ffn_w.after(d, "weight"))
                    dve.tensor_scalar(y[:, d.parity, 1, :], ps[0:HS, 5, :], weight_of[d.parity][:, 1:2],
                                                  None, ALU.mult).then_inc(dwn_v.sem, 1)
                if u.exists():
                    dve.wait_ge(wdn_a.sem, wdn_a.after(u, "high"))
                    left_by(dn_low[:, u.parity, 0, :], dn_sb[:, u.parity, :], dn_high[:, u.parity, 0, :]).then_inc(wdn_v.sem, 1)
                    dve.wait_ge(wdn_a.sem, wdn_a.after(u, "high2"))
                    left_by(dn2_low[0:INTER - P, u.parity, 0, :], dn2_sb[0:INTER - P, u.parity, :],
                                        dn2_high[0:INTER - P, u.parity, 0, :]).then_inc(wdn_v.sem, 1)
                if t.exists():
                    dve.wait_ge(d_rows[t.parity], moved(t, 2))
                    if t.back(2).exists():
                        dve.wait_ge(dwn_a.sem, dwn_a.after(t.back(2), "y0"))
                        dve.wait_ge(dwn_v.sem, dwn_v.after(t.back(2), "y1"))
                    settled(dve)
                    dve.tensor_copy(weight_of[t.parity][:, :],
                                                rows[:, t.parity, :, bass.ds(t.index + DM, 1)]
                                                .rearrange("p h o -> p (h o)")).then_inc(ffn_w.sem, 1)
            expert_turns(dve, expert_turn)

        @block.tensor
        def _(pe):
            def gate_columns():
                pe.wait_ge(setup_v.sem, setup_v.after(once, "new"))
                for c in range(KC):
                    pe.matmul(ps[:, 7, c * E:(c + 1) * E], gate_sb[:, c * P:(c + 1) * P], is_new[:, :],
                              start=True, stop=True)
                pe.matmul(ps[:, 7, KC * E:(KC + 1) * E], ones[:, :], is_new[:, :],
                                        start=True, stop=True).then_inc(setup_t.sem, 1)

            def transpose4(bank, src):
                for c in range(KC):
                    last = pe.transpose(blocks(bank)[:, c, :], src(c), ident[:, :])
                return last

            def product(dst, left, right, n=KC):
                for c in range(n):
                    last = pe.matmul(dst, left(c), right(c), start=(c == 0), stop=(c == n - 1))
                return last

            def product_r(dst, high, low, m, first):
                if first:
                    pe.wait_ge(s_split_v, m + 1)
                parts = [(high, w_high), (high, w_low), (low, w_high)]
                for n, (left, right) in enumerate(parts):
                    for c in range(KC):
                        last = pe.matmul(dst, left[:, c, :], right[:, m, c, :], start=(n == 0 and c == 0),
                                         stop=(n == 2 and c == KC - 1))
                        if n == 1 and c == KC - 1:
                            yield None
                yield last

            def turn(b):
                p, a, c, r = b["project"], b["attend"], b["cross"], b["route"]
                if p.exists():
                    pe.wait_ge(ln1_a.sem, ln1_a.after(p, "normed"))
                    if p.back(1).exists():
                        pe.wait_ge(prj_a.sem, prj_a.after(p.back(1), "kT"))
                    transpose4(bank_ta, lambda k: xn1[:, p.parity, k * P:(k + 1) * P]).then_inc(prj_t.sem, 1)
                if r.first():
                    pe.wait_ge(setup_v.sem, setup_v.after(once, "absent"))
                if a.exists():
                    pe.wait_ge(prj_a.sem, prj_a.after(a, "kT"))
                    pe.wait_ge(prj_a.sem, prj_a.after(a, "v"))
                    if a.back(1).exists():
                        pe.wait_ge(att_a.sem, att_a.after(a.back(1), "exp"))
                    for h in range(H):
                        for s in range(2):
                            half = slice(s * HALF, (s + 1) * HALF)
                            last = pe.matmul(blocks(banks_s[:, s, :])[:, h, :], q_t[half, h, :], k_t[half, h, :],
                                             start=True, stop=True)
                    last.then_inc(att_t.sem, 1)
                if c.exists():
                    pe.wait_ge(att_v.sem, att_v.after(c, "heads"))
                    if a.exists():
                        pe.wait_ge(prj_a.sem, prj_a.after(a, "qT"))
                    transpose4(bank_tb, lambda k: heads[:, k, :]).then_inc(hds_t.sem, 1)
                if p.exists():
                    if p.back(1).exists():
                        pe.wait_ge(rope.sem, rope.after(p.back(1), "sin"))
                    q = product_r(banks_qk[:, 0, :], xn1_high, xn1_low, W_Q, p.first())
                    pe.wait_ge(prj_a.sem, prj_a.after(p, "xT"))
                    next(q)
                if c.exists():
                    pe.wait_ge(hds_a.sem, hds_a.after(c, "high"))
                    proj = product_r(bank_o, heads_high, heads_low, W_OUT, c.first())
                    next(proj)
                    pe.wait_ge(att_l.sem, att_l.after(c, "low"))
                    next(proj).then_inc(att_o.sem, 1)
                if p.exists():
                    pe.wait_ge(prj_v.sem, prj_v.after(p, "low"))
                    next(q).then_inc(prj_t.sem, 1)
                if r.exists():
                    pe.wait_ge(out_v.sem, out_v.after(r, "normed"))
                    if c.exists():
                        pe.wait_ge(hds_a.sem, hds_a.after(c, "headsT"))
                    transpose4(bank_tb, lambda k: row[:, r.parity, k * P:(k + 1) * P]).then_inc(rte_t.sem, 1)
                if p.exists():
                    k = product_r(banks_qk[:, 1, :], xn1_high, xn1_low, W_K, p.first())
                    next(k)
                    next(k).then_inc(prj_t.sem, 1)
                if c.exists():
                    pe.wait_ge(crs_v.sem, crs_v.after(c, "normed"))
                    if p.exists():
                        pe.wait_ge(prj_v.sem, prj_v.after(p, "low"))
                    transpose4(bank_ta, lambda k: xn2[:, k * P:(k + 1) * P]).then_inc(crs_t.sem, 1)
                if r.exists():
                    pe.wait_ge(rte_a.sem, rte_a.after(r, "xT"))
                    pe.wait_ge(out_v.sem, out_v.after(r, "x2"))
                    product(logit_ps, lambda k: xn3_t[:, k, :], lambda k: gate_new[:, k, :]).then_inc(rte_t.sem, 1)
                if c.exists():
                    pe.wait_ge(crs_a.sem, crs_a.after(c, "xT"))
                    pe.wait_ge(d_ctx[c.parity], moved(c, 2))
                    product(xscore_ps, lambda k: xn2_t[:, k, :], lambda k: ctx_t_sb[:, c.parity, k, :]).then_inc(crs_t.sem, 1)
                if a.exists():
                    pe.wait_ge(att_v.sem, att_v.after(a, "diff"))
                    if r.exists():
                        pe.wait_ge(rte_a.sem, rte_a.after(r, "xT"))
                    transpose4(bank_tb, lambda k: diff[:, k, :]).then_inc(att_t.sem, 1)
                if p.exists():
                    if a.exists():
                        pe.wait_ge(att_a.sem, att_a.after(a, "exp"))
                    v = product_r(bank_v, xn1_high, xn1_low, W_V, p.first())
                    next(v)
                if a.exists():
                    pe.wait_ge(att_a.sem, att_a.after(a, "diffT"))
                    if c.exists():
                        pe.wait_ge(crs_v.sem, crs_v.after(c, "x1"))
                    for h in range(H):
                        last = pe.matmul(blocks(bank_o)[:, h, :], diff_t[:, h, :],
                                         v_sb[:, a.parity, h * P:(h + 1) * P], start=True, stop=True)
                    last.then_inc(att_t.sem, 1)
                if p.exists():
                    next(v).then_inc(prj_t.sem, 1)
                if r.exists():
                    pe.wait_ge(rte_v.sem, rte_v.after(r, "chosen"))
                    if c.exists():
                        pe.wait_ge(crs_v.sem, crs_v.after(c, "kept"))
                    pe.matmul(count_ps[:, 0:E], before_bf[:, :], chosen[:, :], start=True, stop=True)
                    pe.matmul(count_ps[:, E:2 * E], ones_bf[:, :], chosen[:, :], start=True, stop=True).then_inc(rte_t.sem, 1)
                if c.exists():
                    pe.wait_ge(crs_a.sem, crs_a.after(c, "exp"))
                    pe.transpose(bank_ta[:, 0:P], xprobs[:, :], ident[:, :]).then_inc(crs_t.sem, 1)
                if p.exists():
                    pe.wait_ge(rope.sem, rope.after(p, "real"))
                    pe.wait_ge(rope_p.sem, rope_p.after(p, "imag"))
                    if a.exists():
                        pe.wait_ge(att_a.sem, att_a.after(a, "diffT"))
                    rot = qk_rot[:, :, :, :].rearrange("p g r f -> p (g r f)")
                    transpose4(bank_tb, lambda k: rot[:, k * P:(k + 1) * P]).then_inc(prj_t.sem, 1)
                    if c.exists():
                        pe.wait_ge(crs_a.sem, crs_a.after(c, "probsT"))
                    transpose4(bank_ta, lambda k: rot[:, DM + k * P:DM + (k + 1) * P]).then_inc(prj_t.sem, 1)
                if c.exists():
                    pe.wait_ge(crs_a.sem, crs_a.after(c, "probsT"))
                    if r.exists():
                        pe.wait_ge(rte_v.sem, rte_v.after(r, "taken"))
                    pe.matmul(bank_r, xprobs_t[:, :], ctx_sb[:, c.parity, :], start=True, stop=True).then_inc(crs_t.sem, 1)
                if c.first():
                    if a.exists():
                        pe.wait_ge(att_a.sem, att_a.after(a, "exp"))
                    gate_columns()
            turns(pe, turn)

            def expert_turn(b):
                t, u, d = b["turn"], b["up"], b["down"]
                if u.exists():
                    pe.wait_ge(wgu_v.sem, wgu_v.after(u, "low"))
                    pe.wait_ge(ffn_v.sem, ffn_v.after(u, "low1"))
                    if u.back(1).exists():
                        pe.wait_ge(gup_v.sem, gup_v.after(u.back(1), "h2"))

                    def gate_up_block(dst, m):
                        cols = slice(m * P, (m + 1) * P)
                        pairs = [(gu_high, rows_high), (gu_high, rows_low), (gu_low, rows_high)]
                        for n, (left, right) in enumerate(pairs):
                            for k in range(KC):
                                last = pe.matmul(dst, left[:, u.parity, k, cols], right[:, u.parity, k, :],
                                                 start=(n == 0 and k == 0), stop=(n == 2 and k == KC - 1))
                        return last
                    for m in range(2):
                        last = gate_up_block(ps[:, 2, m * CAP:(m + 1) * CAP], m)
                    last.then_inc(gup_t.sem, 1)
                    gate_up_block(ps[:, 3, 0:CAP], 2).then_inc(gup_t.sem, 1)
                if t.exists():
                    pe.wait_ge(d_rows[t.parity], moved(t, 2))
                    for h in range(2):
                        if t.back(1).exists():
                            pe.wait_ge(ffn_v.sem, ffn_v.after(t.back(1), f"low{h}"))
                        for c in range(KC):
                            last = pe.transpose(ps[:, h, c * HS:(c + 1) * HS], rows[:, t.parity, h, c * P:(c + 1) * P],
                                                ident[0:HS, 0:HS])
                        last.then_inc(ffn_t.sem, 1)
                if d.exists():
                    pe.wait_ge(wdn_v.sem, wdn_v.after(d, "low2"))
                    pe.wait_ge(gup_v.sem, gup_v.after(d, "low2"))
                    for h in range(2):
                        if h == 0:
                            if d.back(1).exists():
                                pe.wait_ge(dwn_a.sem, dwn_a.after(d.back(1), "y0"))
                        else:
                            if d.back(1).exists():
                                pe.wait_ge(dwn_v.sem, dwn_v.after(d.back(1), "y1"))
                        half = slice(h * HS, (h + 1) * HS)
                        dst = ps[0:HS, 4 + h, :]
                        pairs = [(h1_high, dn_high, P), (h1_high, dn_low, P), (h1_low, dn_high, P),
                                 (h2_both, dn2_high, P), (h2_high, dn2_low, INTER - P)]
                        for i, (left, right, n) in enumerate(pairs):
                            last = pe.matmul(dst, left[:, d.parity, 0, half], right[0:n, d.parity, 0, :],
                                             start=(i == 0), stop=(i == len(pairs) - 1))
                        last.then_inc(dwn_t.sem, 1)
            expert_turns(pe, expert_turn)


def kernel(x, ctx_2048, mask_BxS2_bk0, L0_attn_wq, L0_attn_wk, L0_attn_wv, L0_attn_wout, L0_attn_lambda_q1,
           L0_attn_lambda_q2, L0_attn_lambda_k1, L0_attn_lambda_k2, L0_attn_subln_weight, L0_ffn_gate_weight,
           L0_ffn_gate_up_proj, L0_ffn_down_proj, L0_ffn_old_to_new):
    import concourse.bacc as bacc
    from concourse.bass_utils import run_bass_kernel_spmd

    f = lambda a: np.ascontiguousarray(np.asarray(a))

    def chunked(w):
        return w.T.reshape(w.shape[1] // P, P, w.shape[0]).transpose(1, 0, 2)

    def halves(w):
        return w.reshape(NH2, NF, 2, DM).transpose(0, 2, 1, 3).reshape(DM, DM)

    wq, wk = halves(f(L0_attn_wq)), halves(f(L0_attn_wk))
    gu = f(L0_ffn_gate_up_proj)
    g, u = gu[:, :INTER], gu[:, INTER:]
    gu = np.concatenate([g[:, :P], u[:, :P], g[:, P:], u[:, P:]], axis=1)
    gu = gu.transpose(0, 2, 1).reshape(E, KC, P, 2 * INTER).transpose(0, 2, 1, 3).reshape(E * P, KC, 2 * INTER)
    ctx = f(ctx_2048)
    angle = np.outer(np.arange(P), 1.0 / 10000.0 ** (np.arange(0, HALF, 2).astype(np.float64) / HALF))
    arrays = {
        "x": f(x).reshape(T, DM),
        "ctx_rows": ctx.reshape(NB * M, DM),
        "ctx_t": ctx.transpose(0, 2, 1).reshape(NB, KC, P, M).transpose(0, 2, 1, 3).reshape(NB * P, KC, M),
        "mask": f(mask_BxS2_bk0).reshape(NB * M),
        "weights": np.concatenate([chunked(w) for w in (wq, wk, f(L0_attn_wv), f(L0_attn_wout))]),
        "lambda_q1": f(L0_attn_lambda_q1),
        "lambda_q2": f(L0_attn_lambda_q2),
        "lambda_k1": f(L0_attn_lambda_k1),
        "lambda_k2": f(L0_attn_lambda_k2),
        "subln": f(L0_attn_subln_weight),
        "gate": f(L0_ffn_gate_weight),
        "gate_up": gu,
        "down_proj": f(L0_ffn_down_proj).transpose(0, 2, 1).reshape(E * INTER, DM),
        "old_to_new": f(L0_ffn_old_to_new),
        "cos_sin": np.stack([np.cos(angle), np.sin(angle)], axis=1).astype(np.float32),
    }
    arrays = {k: np.ascontiguousarray(v) for k, v in arrays.items()}
    nc = bacc.Bacc("TRN2", target_bir_lowering=False, num_devices=1)
    ap = {k: nc.dram_tensor(f"in_{k}", v.shape, mybir.dt.from_np(v.dtype), kind="ExternalInput").ap()
          for k, v in arrays.items()}
    out = nc.dram_tensor("layer_out", (T + CAP, DM), FP32, kind="ExternalOutput").ap()
    lambdas = [ap.pop(k) for k in ("lambda_q1", "lambda_q2", "lambda_k1", "lambda_k2")]
    decoder_layer(nc, lambdas=lambdas, out=out, **ap)
    result = run_bass_kernel_spmd(nc, [{f"in_{k}": v for k, v in arrays.items()}], core_ids=[0])
    return np.asarray(result.results[0]["layer_out"])[:T].reshape(NB, P, DM)
```
